# Optimizing a Trainium2 kernel written in Bass

```python
import numpy as np
import jax
import jax.numpy as jnp

def _softmax(x, axis=-1):
    return jax.nn.softmax(x, axis=axis)

def _gelu(x):
    return jax.nn.gelu(x, approximate=True)

def _silu(x):
    return jax.nn.silu(x)

def _sigmoid(x):
    return jax.nn.sigmoid(x)

def _layernorm(x, axis=-1, eps=1e-05):
    m = jnp.mean(x, axis=axis, keepdims=True)
    v = jnp.var(x, axis=axis, keepdims=True)
    return (x - m) / jnp.sqrt(v + eps)

def _scatter_add(tgt, idx, src, axis=0):
    return tgt.at[idx].add(src)

def _segment_sum(src, seg, n):
    return jax.ops.segment_sum(src, seg, n)
kernel_name = 'mk_xattn_seq_d2_seqx_r8_f318a0'

def setup_inputs(seed: int=0):
    np.random.seed(seed)
    _w = jnp.asarray

    def _rec_inputs():
        import jax
        import jax.numpy as jnp
        _rk = jax.random.key(seed)
        x = -0.0002928 + 1 * jax.random.normal(jax.random.fold_in(_rk, 1), (64, 64, 128), jnp.float32)
        _lenS = 64 - jax.random.randint(jax.random.fold_in(_rk, 7), (64,), 0, max(1, 64 // 4) + 1, jnp.int32)
        _lenS2 = 64 - jax.random.randint(jax.random.fold_in(_rk, 8), (64,), 0, max(1, 64 // 4) + 1, jnp.int32)
        _ctx_1024P = jax.random.normal(jax.random.fold_in(_rk, 11), (64, 16, 128), jnp.float32)
        _ctx_1024c = jax.random.dirichlet(jax.random.fold_in(_rk, 511), 0.3 * jnp.ones((16,), jnp.float32), (64, 64))
        _ctx_1024t = jnp.einsum('bsk,bkd->bsd', _ctx_1024c, _ctx_1024P)
        _ctx_1024t = _ctx_1024t * jax.lax.rsqrt(jnp.mean(jnp.square(_ctx_1024t)) + 1e-12) * 0.953939
        ctx_1024 = 0.000227908 + 0.99994 * (_ctx_1024t + 0.3 * jax.random.normal(jax.random.fold_in(_rk, 611), (64, 64, 128), jnp.float32))
        _validS = jnp.arange(64)[None, :] < _lenS[:, None]
        _validS2 = jnp.arange(64)[None, :] < _lenS2[:, None]
        _causal = jnp.tril(jnp.ones((64, 64), dtype=bool))
        mask_BxS2_ik0 = jnp.where(jnp.broadcast_to(_validS2[:, :], (64, 64)), 0, 1).astype(jnp.int32)
        return (x, ctx_1024, mask_BxS2_ik0)
    x, ctx_1024, mask_BxS2_ik0 = _rec_inputs()

    def _L0_xattn_setup():
        import jax, jax.numpy as jnp
        import numpy as np
        B, T, S, D, H, F = (2, 256, 64, 128, 16, 512)
        DH = D // H
        EPS = 1e-05

        def _ln(x, g, b):
            m = x.mean(-1, keepdims=True)
            v = ((x - m) ** 2).mean(-1, keepdims=True)
            return (x - m) * jax.lax.rsqrt(v + EPS) * g + b
        key = jax.random.key(seed)
        ks = jax.random.split(key, 8)
        w = lambda k, shape: jax.random.normal(k, shape, dtype=jnp.float32) * 0.02
        return {'x': jax.random.normal(ks[0], (B, T, D), dtype=jnp.float32), 'context': jax.random.normal(ks[1], (B, S, D), dtype=jnp.float32), 'w_qkv': w(ks[2], (D, 3 * D)), 'b_qkv': jnp.zeros((3 * D,), jnp.float32), 'w_ckv': w(ks[3], (D, 2 * D)), 'b_ckv': jnp.zeros((2 * D,), jnp.float32), 'g1': jnp.ones((D,), jnp.float32), 'be1': jnp.zeros((D,), jnp.float32), 'g2': jnp.ones((D,), jnp.float32), 'be2': jnp.zeros((D,), jnp.float32), 'gf': jnp.ones((D,), jnp.float32), 'bf': jnp.zeros((D,), jnp.float32), 'w1': w(ks[4], (D, F)), 'b1': jnp.zeros((F,), jnp.float32), 'w2': w(ks[5], (F, D)), 'b2': jnp.zeros((D,), jnp.float32)}
    _L0_xattn_all = _L0_xattn_setup()
    _L0_xattn_in = {k: v for k, v in _L0_xattn_all.items() if k in ('w_qkv', 'b_qkv', 'w_ckv', 'b_ckv', 'g1', 'be1', 'g2', 'be2', 'gf', 'bf', 'w1', 'b1', 'w2', 'b2')}
    del _L0_xattn_all

    def _L1_xattn_setup():
        import jax, jax.numpy as jnp
        import numpy as np
        HIDDEN_DIM = 128
        NUM_HEADS = 16
        HEAD_DIM = HIDDEN_DIM // NUM_HEADS
        LN_EPS = 1e-05
        NEG_INF = -1000000000.0

        def _layer_norm(x, w, b):
            mu = jnp.mean(x, axis=-1, keepdims=True)
            var = jnp.mean(jnp.square(x - mu), axis=-1, keepdims=True)
            return (x - mu) * jax.lax.rsqrt(var + LN_EPS) * w + b
        key = jax.random.key(seed)
        ks = jax.random.split(key, 12)
        B, Lq, Lk, D = (4, 128, 256, HIDDEN_DIM)
        s = 1.0 / np.sqrt(D)
        return {'query': jax.random.normal(ks[0], (B, Lq, D), dtype=jnp.float32), 'key_value': jax.random.normal(ks[1], (B, Lk, D), dtype=jnp.float32), 'key_mask': jax.random.randint(ks[2], (B, Lk), 0, 2, dtype=jnp.int32), 'ln_w': jnp.ones((D,), dtype=jnp.float32), 'ln_b': jnp.zeros((D,), dtype=jnp.float32), 'wq': jax.random.normal(ks[3], (D, D), dtype=jnp.float32) * s, 'bq': jnp.zeros((D,), dtype=jnp.float32), 'wk': jax.random.normal(ks[4], (D, D), dtype=jnp.float32) * s, 'bk': jnp.zeros((D,), dtype=jnp.float32), 'wv': jax.random.normal(ks[5], (D, D), dtype=jnp.float32) * s, 'bv': jnp.zeros((D,), dtype=jnp.float32), 'wo': jax.random.normal(ks[6], (D, D), dtype=jnp.float32) * s, 'bo': jnp.zeros((D,), dtype=jnp.float32)}
    _L1_xattn_all = _L1_xattn_setup()
    _L1_xattn_in = {k: v for k, v in _L1_xattn_all.items() if k in ('ln_w', 'ln_b', 'wq', 'bq', 'wk', 'bk', 'wv', 'bv', 'wo', 'bo')}
    del _L1_xattn_all
    return {'x': x, 'ctx_1024': ctx_1024, 'mask_BxS2_ik0': mask_BxS2_ik0, 'L0_xattn_w_qkv': _L0_xattn_in['w_qkv'], 'L0_xattn_b_qkv': _L0_xattn_in['b_qkv'], 'L0_xattn_w_ckv': _L0_xattn_in['w_ckv'], 'L0_xattn_b_ckv': _L0_xattn_in['b_ckv'], 'L0_xattn_g1': _L0_xattn_in['g1'], 'L0_xattn_be1': _L0_xattn_in['be1'], 'L0_xattn_g2': _L0_xattn_in['g2'], 'L0_xattn_be2': _L0_xattn_in['be2'], 'L0_xattn_gf': _L0_xattn_in['gf'], 'L0_xattn_bf': _L0_xattn_in['bf'], 'L0_xattn_w1': _L0_xattn_in['w1'], 'L0_xattn_b1': _L0_xattn_in['b1'], 'L0_xattn_w2': _L0_xattn_in['w2'], 'L0_xattn_b2': _L0_xattn_in['b2'], 'L1_xattn_ln_w': _L1_xattn_in['ln_w'], 'L1_xattn_ln_b': _L1_xattn_in['ln_b'], 'L1_xattn_wq': _L1_xattn_in['wq'], 'L1_xattn_bq': _L1_xattn_in['bq'], 'L1_xattn_wk': _L1_xattn_in['wk'], 'L1_xattn_bk': _L1_xattn_in['bk'], 'L1_xattn_wv': _L1_xattn_in['wv'], 'L1_xattn_bv': _L1_xattn_in['bv'], 'L1_xattn_wo': _L1_xattn_in['wo'], 'L1_xattn_bo': _L1_xattn_in['bo']}

def reference(x, ctx_1024, mask_BxS2_ik0, L0_xattn_w_qkv, L0_xattn_b_qkv, L0_xattn_w_ckv, L0_xattn_b_ckv, L0_xattn_g1, L0_xattn_be1, L0_xattn_g2, L0_xattn_be2, L0_xattn_gf, L0_xattn_bf, L0_xattn_w1, L0_xattn_b1, L0_xattn_w2, L0_xattn_b2, L1_xattn_ln_w, L1_xattn_ln_b, L1_xattn_wq, L1_xattn_bq, L1_xattn_wk, L1_xattn_bk, L1_xattn_wv, L1_xattn_bv, L1_xattn_wo, L1_xattn_bo):
    import jax
    import jax.numpy as jnp

    def _L0_xattn_ref(x, context, w_qkv, b_qkv, w_ckv, b_ckv, g1, be1, g2, be2, gf, bf, w1, b1, w2, b2):
        import jax, jax.numpy as jnp
        import numpy as np
        B, T, S, D, H, F = (2, 256, 64, 128, 16, 512)
        DH = D // H
        EPS = 1e-05

        def _ln(x, g, b):
            m = x.mean(-1, keepdims=True)
            v = ((x - m) ** 2).mean(-1, keepdims=True)
            return (x - m) * jax.lax.rsqrt(v + EPS) * g + b
        b, t, d = x.shape
        s = context.shape[1]
        h, dh = (H, d // H)
        qkv = (_ln(x, g1, be1) @ w_qkv + b_qkv).reshape(b, t, 3, h, dh)
        q, k_self, v_self = (qkv[:, :, 0], qkv[:, :, 1], qkv[:, :, 2])
        ckv = (context @ w_ckv + b_ckv).reshape(b, s, 2, h, dh)
        k_ctx, v_ctx = (ckv[:, :, 0], ckv[:, :, 1])
        k = jnp.concatenate([k_self, k_ctx], axis=1)
        v = jnp.concatenate([v_self, v_ctx], axis=1)
        scale = 1.0 / jnp.sqrt(jnp.float32(dh))
        scores = jnp.einsum('bthd,bshd->bhts', q, k) * scale
        i = jnp.arange(t)[:, None]
        j = jnp.arange(t + s)[None, :]
        mask = (j >= t) | (j <= i)
        scores = jnp.where(mask, scores, -jnp.inf)
        attn = jax.nn.softmax(scores, axis=-1)
        attn_out = jnp.einsum('bhts,bshd->bthd', attn, v).reshape(b, t, d)
        x = x + attn_out
        hdn = _ln(_ln(x, g2, be2), gf, bf) @ w1 + b1
        hdn = jax.nn.gelu(hdn, approximate=False)
        x = x + (hdn @ w2 + b2)
        return x

    def _L1_xattn_ref(query, key_value, key_mask, ln_w, ln_b, wq, bq, wk, bk, wv, bv, wo, bo):
        import jax, jax.numpy as jnp
        import numpy as np
        HIDDEN_DIM = 128
        NUM_HEADS = 16
        HEAD_DIM = HIDDEN_DIM // NUM_HEADS
        LN_EPS = 1e-05
        NEG_INF = -1000000000.0

        def _layer_norm(x, w, b):
            mu = jnp.mean(x, axis=-1, keepdims=True)
            var = jnp.mean(jnp.square(x - mu), axis=-1, keepdims=True)
            return (x - mu) * jax.lax.rsqrt(var + LN_EPS) * w + b
        B, Lq, D = query.shape
        Lk = key_value.shape[1]
        H, hd = (NUM_HEADS, HEAD_DIM)
        residual = query
        qn = _layer_norm(query, ln_w, ln_b)
        Q = (qn @ wq.T + bq).reshape(B, Lq, H, hd)
        K = (key_value @ wk.T + bk).reshape(B, Lk, H, hd)
        V = (key_value @ wv.T + bv).reshape(B, Lk, H, hd)
        scores = jnp.einsum('bqhd,bkhd->bhqk', Q, K) / np.sqrt(hd)
        scores = jnp.where(key_mask[:, None, None, :] == 0, NEG_INF, scores)
        probs = jax.nn.softmax(scores, axis=-1)
        ctx = jnp.einsum('bhqk,bkhd->bqhd', probs, V).reshape(B, Lq, D)
        out = ctx @ wo.T + bo
        return out + residual
    x = _L0_xattn_ref(x, ctx_1024, L0_xattn_w_qkv, L0_xattn_b_qkv, L0_xattn_w_ckv, L0_xattn_b_ckv, L0_xattn_g1, L0_xattn_be1, L0_xattn_g2, L0_xattn_be2, L0_xattn_gf, L0_xattn_bf, L0_xattn_w1, L0_xattn_b1, L0_xattn_w2, L0_xattn_b2)
    x = _L1_xattn_ref(x, ctx_1024, mask_BxS2_ik0, L1_xattn_ln_w, L1_xattn_ln_b, L1_xattn_wq, L1_xattn_bq, L1_xattn_wk, L1_xattn_bk, L1_xattn_wv, L1_xattn_bv, L1_xattn_wo, L1_xattn_bo)
    return x

_drawn_inputs = setup_inputs


def setup_inputs(seed=0):
    import zlib

    import numpy as np

    out = dict(_drawn_inputs(seed))
    spreads = {'L0_xattn_b_qkv': (0.0, 0.302),
     'L0_xattn_b_ckv': (0.0, 0.1),
     'L0_xattn_g1': (1.0, 0.6),
     'L0_xattn_be1': (0.0, 0.8),
     'L0_xattn_g2': (1.0, 0.6),
     'L0_xattn_be2': (0.0, 2.0),
     'L0_xattn_gf': (1.0, 0.6),
     'L0_xattn_bf': (0.0, 2.0),
     'L0_xattn_b1': (0.0, 0.437),
     'L0_xattn_b2': (0.0, 0.1),
     'L1_xattn_ln_w': (1.0, 0.2),
     'L1_xattn_ln_b': (0.0, 0.295),
     'L1_xattn_bq': (0.0, 0.351),
     'L1_xattn_bk': (0.0, 2.0),
     'L1_xattn_bv': (0.0, 0.1),
     'L1_xattn_bo': (0.0, 0.1)}
    factors = {'L0_xattn_w_qkv': 4.535}
    for name, (base, spread) in spreads.items():
        noise = np.random.default_rng([zlib.crc32(name.encode()), seed]).standard_normal(out[name].shape)
        drawn = base * np.exp(spread * noise) if base else spread * noise
        out[name] = jnp.asarray(drawn.astype(out[name].dtype))
    for name, factor in factors.items():
        out[name] = (out[name] * factor).astype(out[name].dtype)
    return out
```

```python
from contextlib import ExitStack

import concourse.bass as bass
from concourse import mybir

ALU = mybir.AluOpType
ACT = mybir.ActivationFunctionType
AX_X = mybir.AxisListType.X
F32 = mybir.dt.float32
F16 = mybir.dt.float16
BF16 = mybir.dt.bfloat16
I32 = mybir.dt.int32

P = 128
B, T, D = 64, 64, 128
H, DH, F = 16, 8, 512
CB = 16
CHUNKS = B // CB
TOK = CB * T
TILES = TOK // P
HALF = TOK // 2
FC = F // P
G = 4
HG = H // G
PARTS = 2
TERMS = 3
ROWS = TERMS * HG * DH
Q_PART = (0, 0, 1)
K_PART = (0, 1, 0)
PAIRS = H // 2
VW = 16
EPS = 1e-5
SCALE = float(DH) ** -0.5
CAUSAL = -1e30
N_VEC = 11 + FC
KEYMASK = 32768.0

U0, U1 = CB, CB // 2
U = U0 + U1

JOBS_IN = (["act"] * 2 + ["dve"] * 2
           + ["dve"] * 6
           + ["dve"] * 4
           + ["dve"] * 2 + ["dve"] * 2)
JOBS_FFN = (["dve"] + ["act"] * FC + ["dve"]) * 2
JOBS_Q1 = ["dve"] * 4
JOBS_OUT = ["dve"] * 2
JOBS = JOBS_IN + JOBS_FFN + JOBS_Q1 + JOBS_OUT
J_FFN, J_Q1, J_OUT = len(JOBS_IN), len(JOBS_IN + JOBS_FFN), len(JOBS_IN + JOBS_FFN + JOBS_Q1)
JOB_BANKS = 6
ACT_JOBS, DVE_JOBS = JOBS.count("act"), JOBS.count("dve")


def jobs_read(who, n):
    return JOBS[:n].count(who)



def side_uses():
    uses = []
    for first, last in ((0, U0), (U0, U)):
        uses.append(("top", first))
        for u in range(first, last + 1):
            v = u - 2 if u < last else last - 1
            if v > first and v % 2:
                uses += [("nat", v)] + [("back", v)] * (first == U0)
            if u + 1 < last:
                uses.append(("top", u + 1))
    return {use: n for n, use in enumerate(uses)}


SIDE_AT = side_uses()
SIDE = len(SIDE_AT)
STACKED = 16 * TERMS * G

C_ID, C_HH, C_LO, C_BL, C_BF = 0, P, P + HG, P + HG + 2, P + HG + 2 + PAIRS
C_EK, C_EQ, C_HK, C_HQ, C_ST = 0, P, 2 * P, 2 * P + T, 2 * P + 2 * T
CWB = C_ST + 2 * P
CW = C_BF + CWB


def constants():
    import numpy as np

    p = np.arange(P)[:, None]
    c = np.arange(P)[None, :]
    k = np.arange(T)[None, :]
    out = np.zeros((P, CW), np.float32)
    out[:, C_ID:C_ID + P] = p == c
    out[:, C_HH:C_HH + HG] = p % (HG * DH) // DH == np.arange(HG)
    out[:, C_LO:C_LO + 1] = -1.0 * (p // 8 == 1)
    out[:, C_LO + 1:C_LO + 2] = -1.0 * (p // 16 == 1)
    out[:, C_BL:C_BL + PAIRS] = p % PAIRS == np.arange(PAIRS)
    b = out[:, C_BF:]
    b[:, C_EK:C_EK + P] = (p == c) & (p < T)
    b[:, C_EQ:C_EQ + P] = (p == c % T) & (p < T)
    b[:, C_HK:C_HK + T] = np.where((k > p) & (p < T), CAUSAL, 0.0)
    b[:, C_HQ:C_HQ + T] = np.where((p > k) & (p < T), CAUSAL, 0.0)
    b[:, C_ST:C_ST + P] = p < 16
    b[:, C_ST + P:C_ST + 2 * P] = (p < 32) & (p // 8 % 2 == c // T)
    return out


def xattn_program(nc, io, consts, out):
    ctx = ExitStack()
    with ctx:
        def sb(name, shape, dt=F32):
            return ctx.enter_context(nc.sbuf_tensor(name, shape, dt))

        def sem(name):
            return ctx.enter_context(nc.semaphore(name))

        w_qkv = sb("w_qkv", [P, 3 * D])
        w_ckv = sb("w_ckv", [P, 2 * D])
        w1 = sb("w1", [P, F])
        w2 = sb("w2", [P, FC, D])
        w_nat = sb("w_nat", [P, 4, D])
        w_t = sb("w_t", [P, 4, D])
        vectors = sb("vectors", [N_VEC, P])
        cols = sb("cols", [P, N_VEC])
        (G1, BE1, GF, BF, LW, LB, BQ0, BK0, BKC, BQ1, BK1) = range(11)
        B1 = 11
        row_g2 = sb("row_g2", [P, D])
        row_be2 = sb("row_be2", [P, D])
        row_b2 = sb("row_b2", [P, D])
        row_bv0 = sb("row_bv0", [P, D])
        row_bv1 = sb("row_bv1", [P, D])
        row_bo = sb("row_bo", [P, D])
        half = sb("half", [P, TILES])
        cst = sb("cst", [P, CW])
        cstb = sb("cstb", [P, CWB], BF16)
        blocks = sb("blocks", [P, PAIRS, P], BF16)
        hh_mask = cst[:, C_HH:C_HH + HG]
        lo_row = [cst[:, C_LO + n:C_LO + n + 1] for n in (0, 1)]
        eye_key = cstb[:, C_EK:C_EK + P]
        eye_query = cstb[:, C_EQ:C_EQ + P]
        hide_key = cstb[:, C_HK:C_HK + T]
        hide_query = cstb[:, C_HQ:C_HQ + T]
        shift_to = [cstb[:, C_ST + P * n:C_ST + P * n + P] for n in (0, 1)]

        x_in = sb("x_in", [P, TILES, D])
        ctx_in = sb("ctx_in", [P, TILES, D])
        normed = sb("normed", [P, TILES, D])
        normed_t = sb("normed_t", [P, TOK])
        ctx_t = sb("ctx_t", [P, TOK])
        q_part = sb("q_part", [P, PARTS, TOK], F16)
        q_diag = sb("q_diag", [P, PARTS, CB, HG, T], F16)
        k_part = sb("k_part", [P, PARTS, CB, 2, T], F16)
        k1_part = sb("k1_part", [P, PARTS, TOK], F16)
        q_stack = sb("q_stack", [P, G, CB, HG * T], F16)
        k_stack = sb("k_stack", [P, G, CB, 2 * T], F16)
        k1_stack = sb("k1_stack", [P, G, TOK], F16)
        v0 = sb("v0", [P, CB, PAIRS, 2, VW])
        v1 = sb("v1", [P, TILES, H, 2, VW])
        probs = [sb(f"probs{n}", [P, H, T]) for n in (0, 1)]
        shift = [sb(f"shift{n}", [P, PAIRS, P], BF16) for n in (0, 1)]
        top = sb("top", [P, 16])
        top_rep = sb("top_rep", [P, P])
        top_hi = sb("top_hi", [P, P], BF16)
        top_row = sb("top_row", [P, P], BF16)
        stat6 = sb("stat6", [P, TILES, 6])
        mean_var = sb("mean_var", [P, TILES, 2])
        var_eps = sb("var_eps", [P, TILES])
        rstd = sb("rstd", [P, TILES])
        o_t = sb("o_t", [P, 4, 2, T])
        rden = sb("rden", [P, 32])
        o_nat = sb("o_nat", [P, 2, D])
        x1 = sb("x1", [P, TILES, D])
        x2 = sb("x2", [P, TILES, D])
        hidden = sb("hidden", [P, FC, HALF])
        k1_full = hidden
        mix_t = sb("mix_t", [P, TOK])
        mask_in = sb("mask_in", [P, TOK], I32)
        keep = sb("keep", [P, TOK])
        result = normed

        bank = [ctx.enter_context(nc.psum_tensor(f"bank{n}", [P, 512], F32)) for n in range(8)]
        side, mixed = bank[6], bank[7]

        s_const = sem("s_const")
        s_wt = sem("s_wt")
        s_setup = sem("s_setup")
        s_x = sem("s_x")
        s_ctx = sem("s_ctx")
        s_var = sem("s_var")
        s_rstd = sem("s_rstd")
        s_ready = sem("s_ready")
        s_job = sem("s_job")
        s_act_job = sem("s_act_job")
        s_dve_job = sem("s_dve_job")
        s_hi = sem("s_hi")
        s_diag = sem("s_diag")
        s_k1_lo = sem("s_k1_lo")
        s_kst = sem("s_kst")
        s_qst = sem("s_qst")
        s_k1st = sem("s_k1st")
        s_bias = sem("s_bias")
        s_scores_q = sem("s_scores_q")
        s_top = sem("s_top")
        s_side = sem("s_side")
        s_side_read = sem("s_side_read")
        s_shift = sem("s_shift")
        s_scores_k = sem("s_scores_k")
        s_probs = sem("s_probs")
        s_mixed = sem("s_mixed")
        s_o_t = sem("s_o_t")
        s_x1 = sem("s_x1")
        s_stored = sem("s_stored")
        s_step = sem("s_step")

        tokens = lambda a: a.rearrange("(c t b) q d -> c (b q) t d", c=CHUNKS, b=2)
        x_d, ctx_d, out_d = tokens(io["x"]), tokens(io["ctx_1024"]), tokens(out)
        mask_d = io["mask_BxS2_ik0"].rearrange("(c b) k -> c (b k)", c=CHUNKS)
        block = ctx.enter_context(nc.Block())

        def across(v):
            return v.partition_broadcast(P)

        col_of = [("L0_xattn_g1", 0), ("L0_xattn_be1", 0), ("L0_xattn_gf", 0), ("L0_xattn_bf", 0),
                  ("L1_xattn_ln_w", 0), ("L1_xattn_ln_b", 0), ("L0_xattn_b_qkv", 0),
                  ("L0_xattn_b_qkv", D), ("L0_xattn_b_ckv", 0), ("L1_xattn_bq", 0),
                  ("L1_xattn_bk", 0)]
        loads = [(cst[:], consts)]
        loads += [(w_qkv[:], io["L0_xattn_w_qkv"]), (w_ckv[:], io["L0_xattn_w_ckv"]),
                  (w1[:], io["L0_xattn_w1"]),
                  (w2[:], io["L0_xattn_w2"].rearrange("(c p) n -> p c n", p=P))]
        loads += [(w_nat[:, n, :], io[f"L1_xattn_{w}"]) for n, w in enumerate(("wq", "wk", "wv", "wo"))]
        loads += [(vectors[n:n + 1, :], io[v][o:o + D].rearrange("(a p) -> a p", a=1))
                  for n, (v, o) in enumerate(col_of)]
        loads += [(vectors[B1:B1 + FC, :], io["L0_xattn_b1"].rearrange("(c p) -> c p", p=P))]
        loads += [(row_g2[:], across(io["L0_xattn_g2"])), (row_be2[:], across(io["L0_xattn_be2"])),
                  (row_b2[:], across(io["L0_xattn_b2"])), (row_bo[:], across(io["L1_xattn_bo"])),
                  (row_bv1[:], across(io["L1_xattn_bv"])),
                  (row_bv0[0:T], io["L0_xattn_b_qkv"][2 * D:3 * D].partition_broadcast(T)),
                  (row_bv0[T:P], io["L0_xattn_b_ckv"][D:2 * D].partition_broadcast(T))]
        N_CONST = 16 * len(loads)

        @block.sync
        def _(sp):
            for dst, src in loads:
                sp.dma_start(dst, src).then_inc(s_const, 16)
            with sp.Fori(0, CHUNKS) as c:
                sp.wait_ge(s_x1, c * TILES)
                sp.dma_start(ctx_in[:], ctx_d[c]).then_inc(s_ctx, 16)
                sp.dma_start(x_in[:], x_d[c]).then_inc(s_x, 16)
                sp.dma_start(mask_in[:], mask_d[c].partition_broadcast(P)).then_inc(s_x, 16)

                def fill(stack, part, order, filled):
                    for t in range(TERMS):
                        for g in range(G):
                            rows = slice(HG * DH * g, HG * DH * (g + 1))
                            sp.dma_start(stack[HG * DH * t:HG * DH * (t + 1), g],
                                         part[rows, order[t]]).then_inc(filled, 16)

                sp.wait_ge(s_dve_job, c * DVE_JOBS + jobs_read("dve", 8))
                fill(k_stack, k_part[:].rearrange("p a b s k -> p a b (s k)"), K_PART, s_kst)
                sp.wait_ge(s_diag, c * 2 + 1)
                fill(q_stack, q_diag[:].rearrange("p a b h q -> p a b (h q)"), Q_PART, s_qst)
                sp.wait_ge(s_k1_lo, c + 1)
                fill(k1_stack, k1_part, K_PART, s_k1st)
                sp.wait_ge(s_diag, c * 2 + 2)
                fill(q_stack, q_diag[:].rearrange("p a b h q -> p a b (h q)"), Q_PART, s_qst)
                sp.wait_ge(s_dve_job, c * DVE_JOBS + DVE_JOBS)
                sp.dma_start(out_d[c], result[:]).then_inc(s_stored, 16)
            sp.wait_ge(s_stored, 16 * CHUNKS)

        @block.gpsimd
        def _(pool):
            fills = [(half[:], -0.5), (v0[:], 0.0), (v1[:], 0.0), (k1_stack[ROWS:P], 0.0), (q_stack[ROWS:P], 0.0),
                     (v0[:, :, :, :, DH:DH + 1], 1.0), (v1[0:T, :, :, 0, DH:DH + 1], 1.0),
                     (v1[T:P, :, :, 1, DH:DH + 1], 1.0), (q_stack[ROWS:ROWS + 1], KEYMASK)]
            for n, (dst, value) in enumerate(fills):
                nc.gpsimd.memset(dst, value).then_inc(s_setup, 1)
                pool.wait_ge(s_setup, n + 1)
            with pool.Fori(0, CHUNKS) as c:
                for n in range(4):
                    pool.wait_ge(s_var, c * 4 + n + 1)
                    nc.gpsimd.tensor_tensor(rstd[:], var_eps[:], half[:], ALU.pow).then_inc(s_rstd, 1)

        @block.scalar
        def _(act):
            act.wait_ge(s_wt, 1)
            nc.scalar.copy(w_t[:].rearrange("p w n -> p (w n)"), bank[0][:])
            nc.scalar.copy(cols[:], bank[1][:, 0:N_VEC]).then_inc(s_act_job, 1)

            def job(c, n):
                act.wait_ge(s_job, c * len(JOBS) + n + 1)
                return bank[n % JOB_BANKS]

            def high(c, n, out, bias):
                nc.scalar.activation(out, job(c, n)[:], ACT.Identity, bias=bias).then_inc(s_hi, 1)

            def attention(c, u):
                if u < U:
                    act.wait_ge(s_scores_k, c * U + u + 1)
                    if u >= 2:
                        act.wait_ge(s_mixed, c * U + u - 1)
                    for n in (0, 1):
                        ins = nc.scalar.activation(
                            probs[u % 2][:, 8 * n:8 * n + 8].rearrange("p h q -> p (h q)"),
                            bank[2 + 2 * (u % 2) + n][:], ACT.Exp, scale=SCALE)
                    ins.then_inc(s_probs, 1)

            def copy_mixed(c, u):
                act.wait_ge(s_mixed, c * U + u + 1)
                act.wait_ge(s_side, c * SIDE + (SIDE_AT["nat", u - 1 - u % 2] + 1 if u > 1 else 0))
                if u < U0:
                    out = o_t[:, :, u % 2, :].rearrange("p (s a) q -> p a s q", s=2)
                    src = mixed[:, 0:256].rearrange("p (a s q) -> p a s q", a=2, s=2)
                else:
                    out = o_t[:, :, u % 2, :]
                    src = mixed[:, 0:256].rearrange("p (g q) -> p g q", g=G)
                nc.scalar.copy(out, src).then_inc(s_o_t, 1)

            with act.Fori(0, CHUNKS) as c:
                for n in (0, 1):
                    nc.scalar.copy(ctx_t[:, n * HALF:(n + 1) * HALF], job(c, n)[:]).then_inc(s_act_job, 1)
                act.wait_ge(s_kst, c * STACKED)
                act.wait_ge(s_qst, c * 2 * STACKED)
                act.wait_ge(s_k1st, c * STACKED)
                for n in (0, 1):
                    nc.scalar.activation(
                        k_part[:, 0, 8 * n:8 * n + 8, 1, :],
                        job(c, 4 + n)[:].rearrange("p (b k) -> p b k", k=T), ACT.Identity,
                        bias=cols[:, BKC:BKC + 1]).then_inc(s_hi, 1)
                for n in (0, 1):
                    nc.scalar.activation(
                        k_part[:, 0, 8 * n:8 * n + 8, 0, :],
                        job(c, 6 + n)[:].rearrange("p (b k) -> p b k", k=T), ACT.Identity,
                        bias=cols[:, BK0:BK0 + 1]).then_inc(s_hi, 1)
                for n in (0, 1):
                    high(c, 8 + n, q_part[:, 0, n * HALF:(n + 1) * HALF], cols[:, BQ0:BQ0 + 1])
                for n in (0, 1):
                    act.wait_ge(s_dve_job, c * DVE_JOBS + jobs_read("dve", 15 + n))
                    nc.scalar.copy(k1_part[:, 0, n * HALF:(n + 1) * HALF], k1_full[:, n, :]).then_inc(s_hi, 1)
                for u in range(U0):
                    attention(c, u)
                    if u:
                        copy_mixed(c, u - 1)
                copy_mixed(c, U0 - 1)
                for h in (0, 1):
                    for f in range(FC):
                        if h:
                            act.wait_ge(s_job, c * len(JOBS) + J_FFN + 6)
                        nc.scalar.activation(hidden[:, f, :], job(c, J_FFN + 6 * h + 1 + f)[:], ACT.Gelu,
                                             bias=cols[:, B1 + f:B1 + f + 1]).then_inc(s_act_job, 1)
                for n in (0, 1):
                    act.wait_ge(s_qst, c * 2 * STACKED + STACKED)
                    high(c, J_Q1 + 2 + n, q_part[:, 0, n * HALF:(n + 1) * HALF], cols[:, BQ1:BQ1 + 1])
                for u in range(U0, U):
                    attention(c, u)
                    if u > U0:
                        copy_mixed(c, u - 1)
                copy_mixed(c, U - 1)

        @block.tensor
        def _(pe):
            pe.wait_ge(s_const, N_CONST)
            for n in range(4):
                ins = nc.tensor.transpose(bank[0][:, n * D:(n + 1) * D], w_nat[:, n, :], cst[:, C_ID:C_ID + P])
            ins = nc.tensor.transpose(bank[1][:, 0:N_VEC], vectors[:], cst[0:N_VEC, C_ID:C_ID + N_VEC])
            ins.then_inc(s_wt, 1)
            identity = cst[:, C_ID:C_ID + P]

            def open_job(c, n, first):
                if n - first < JOB_BANKS:
                    return bank[n % JOB_BANKS]
                who = JOBS[n - JOB_BANKS]
                per, s = (ACT_JOBS, s_act_job) if who == "act" else (DVE_JOBS, s_dve_job)
                extra = 1 if who == "act" else 0
                pe.wait_ge(s, c * per + extra + jobs_read(who, n - JOB_BANKS + 1))
                return bank[n % JOB_BANKS]

            def all_read(c, n):
                pe.wait_ge(s_act_job, c * ACT_JOBS + 1 + jobs_read("act", n))
                pe.wait_ge(s_dve_job, c * DVE_JOBS + jobs_read("dve", n))

            def transpose4(c, n, src, first):
                b = open_job(c, n, first)
                for i in range(4):
                    ins = nc.tensor.transpose(b[:, i * P:(i + 1) * P], src(i), identity)
                ins.then_inc(s_job, 1)

            def product(c, n, w, src, h, first):
                b = open_job(c, n, first)
                nc.tensor.matmul(b[:], w, src[:, h * HALF:(h + 1) * HALF], start=True,
                                 stop=True).then_inc(s_job, 1)

            def by_query(c, u):
                if u != 0 and u != U0:
                    pe.wait_ge(s_top, c * U + u)
                for n in (0, 1):
                    if u < U0:
                        nc.tensor.matmul(
                            bank[n][:].rearrange("p (a k) -> p a k", a=4)[:, :, 0:T], eye_query,
                            hide_key.unsqueeze(1).broadcast_to([P, 4, T]), start=True, stop=False,
                            skip_group_check=True)
                        for a in range(4):
                            g, two = 2 * n + a // 2, a % 2
                            ins = nc.tensor.matmul(
                                bank[n][:, a * P:(a + 1) * P],
                                q_stack[0:ROWS, g, u, 2 * T * two:2 * T * two + 2 * T],
                                k_stack[0:ROWS, g, u, :], start=False, stop=(a == 3),
                                skip_group_check=True)
                    else:
                        b = 2 * (u - U0) + n
                        for a in range(8):
                            ins = nc.tensor.matmul(
                                bank[n][:, a * T:(a + 1) * T],
                                q_stack[:, a // 2, b, 2 * T * (a % 2):2 * T * (a % 2) + 2 * T],
                                k1_stack[:, a // 2, b * T:(b + 1) * T], start=(a == 0), stop=(a == 7),
                                skip_group_check=True)
                ins.then_inc(s_scores_q, 1)

            def by_key(c, u):
                if u not in (0, 1, U0, U0 + 1):
                    pe.wait_ge(s_probs, c * U + u - 1)
                dst = [bank[2 + 2 * (u % 2)], bank[3 + 2 * (u % 2)]]
                for n in (0, 1):
                    if u < U0:
                        nc.tensor.matmul(dst[n][:], eye_key, hide_query.unsqueeze(1).broadcast_to([P, 8, T]),
                                         start=True, stop=False, skip_group_check=True)
                        for i in (0, 1):
                            nc.tensor.matmul(dst[n][:, 256 * i:256 * i + 256], k_stack[0:ROWS, 2 * n + i, u, :],
                                             q_stack[0:ROWS, 2 * n + i, u, :], start=False, stop=False,
                                             skip_group_check=True)
                    else:
                        for i in (0, 1):
                            for s in (0, 1):
                                b = 2 * (u - U0) + s
                                nc.tensor.matmul(
                                    dst[n][T * s:T * s + T, 256 * i:256 * i + 256],
                                    k1_stack[:, 2 * n + i, b * T:(b + 1) * T], q_stack[:, 2 * n + i, b, :],
                                    start=(i == 0), stop=False, skip_group_check=True)
                pe.wait_ge(s_shift, c * U + u + 1)
                for n in (0, 1):
                    ins = nc.tensor.matmul(
                        dst[n][:], shift_to[u >= U0],
                        shift[u % 2][:, 4 * n:4 * n + 4, :].rearrange("p a q -> p (a q)"),
                        start=False, stop=True, skip_group_check=True)
                ins.then_inc(s_scores_k, 1)

            def top_to_rows(c, u):
                pe.wait_ge(s_top, c * U + u + 1)
                pe.wait_ge(s_side_read, c * SIDE + SIDE_AT["top", u])
                nc.tensor.transpose(side[:, 0:P], top_rep[:], identity).then_inc(s_side, 1)

            def values(c, u):
                pe.wait_ge(s_probs, c * U + u + 1)
                pe.wait_ge(s_o_t, c * U + u)
                pr = probs[u % 2]
                if u < U0:
                    for p in range(PAIRS):
                        j, a = p % 4, p // 4
                        ins = nc.tensor.matmul(
                            mixed[32 * j:32 * j + 32, P * a:P * a + P],
                            v0[:, u, p].rearrange("p s w -> p (s w)"), pr[:, p:H:PAIRS, :],
                            start=True, stop=True)
                else:
                    for h in range(H):
                        j, g = h % 4, h // 4
                        ins = nc.tensor.matmul(
                            mixed[32 * j:32 * j + 32, T * g:T * g + T],
                            v1[:, u - U0, h].rearrange("p s w -> p (s w)"), pr[:, h, :],
                            start=True, stop=True)
                ins.then_inc(s_mixed, 1)

            def to_tokens(c, u):
                pe.wait_ge(s_o_t, c * U + u + 1)
                pe.wait_ge(s_side_read, c * SIDE + SIDE_AT["nat", u])
                for i in range(4):
                    ins = nc.tensor.transpose(side[:, i * P:(i + 1) * P], o_t[:, i].rearrange("p b q -> p (b q)"),
                                              identity)
                ins.then_inc(s_side, 1)

            def to_features(c, u):
                pe.wait_ge(s_side_read, c * SIDE + SIDE_AT["back", u])
                for s in (0, 1):
                    ins = nc.tensor.transpose(side[:, s * P:(s + 1) * P], o_nat[:, s, :], identity)
                ins.then_inc(s_side, 1)

            def attention(c, first, last):
                by_query(c, first)
                top_to_rows(c, first)
                for u in range(first, last):
                    if u + 1 < last:
                        by_query(c, u + 1)
                    by_key(c, u)
                    pair = u - 2 if u - 2 > first and u % 2 else None
                    if pair is not None:
                        to_tokens(c, pair)
                    if u > first:
                        values(c, u - 1)
                    if pair is not None and first == U0:
                        to_features(c, pair)
                    if u + 1 < last:
                        top_to_rows(c, u + 1)
                values(c, last - 1)
                to_tokens(c, last - 1)
                if first == U0:
                    to_features(c, last - 1)

            with pe.Fori(0, CHUNKS) as c:
                pe.wait_ge(s_act_job, c * ACT_JOBS + 1)
                pe.wait_ge(s_dve_job, c * DVE_JOBS)
                pe.wait_ge(s_ctx, c * 16 + 16)
                for n in (0, 1):
                    transpose4(c, n, lambda i, n=n: ctx_in[:, 4 * n + i, :], 0)
                pe.wait_ge(s_ready, c * 3 + 1)
                for n in (0, 1):
                    transpose4(c, 2 + n, lambda i, n=n: normed[:, 4 * n + i, :], 0)
                pe.wait_ge(s_act_job, c * ACT_JOBS + 1 + 2)
                for h in (0, 1):
                    product(c, 4 + h, w_ckv[:, 0:D], ctx_t, h, 0)
                pe.wait_ge(s_dve_job, c * DVE_JOBS + 2)
                for h in (0, 1):
                    product(c, 6 + h, w_qkv[:, D:2 * D], normed_t, h, 0)
                for h in (0, 1):
                    product(c, 8 + h, w_qkv[:, 0:D], normed_t, h, 0)
                for n in range(4):
                    b = open_job(c, 10 + n, 0)
                    for i in range(4):
                        at = slice((4 * n + i) * T, (4 * n + i + 1) * T)
                        nc.tensor.matmul(b[0:T, i * D:(i + 1) * D], normed_t[:, at], w_qkv[:, 2 * D:3 * D],
                                         start=True, stop=True)
                        ins = nc.tensor.matmul(b[T:P, i * D:(i + 1) * D], ctx_t[:, at], w_ckv[:, D:2 * D],
                                               start=True, stop=True)
                    ins.then_inc(s_job, 1)
                for h in (0, 1):
                    product(c, 14 + h, w_t[:, 1, :], ctx_t, h, 0)
                for n in (0, 1):
                    b = open_job(c, 16 + n, 0)
                    for i in range(4):
                        at = slice((4 * n + i) * P, (4 * n + i + 1) * P)
                        ins = nc.tensor.matmul(b[:, i * D:(i + 1) * D], ctx_t[:, at], w_t[:, 2, :],
                                               start=True, stop=True)
                    ins.then_inc(s_job, 1)
                all_read(c, J_FFN)
                pe.wait_ge(s_kst, c * STACKED + STACKED)
                pe.wait_ge(s_qst, c * 2 * STACKED + STACKED)
                attention(c, 0, U0)
                pe.wait_ge(s_probs, c * U + U0)
                pe.wait_ge(s_top, c * U + U0)
                for h in (0, 1):
                    n = J_FFN + 6 * h
                    pe.wait_ge(s_ready, c * 3 + 2)
                    transpose4(c, n, lambda i, h=h: normed[:, 4 * h + i, :], J_FFN)
                    pe.wait_ge(s_dve_job, c * DVE_JOBS + jobs_read("dve", n + 1))
                    for f in range(FC):
                        product(c, n + 1 + f, w1[:, f * P:(f + 1) * P], normed_t, h, J_FFN)
                    b = open_job(c, n + 5, J_FFN)
                    pe.wait_ge(s_act_job, c * ACT_JOBS + 1 + jobs_read("act", n + 5))
                    for i in range(4):
                        for f in range(FC):
                            ins = nc.tensor.matmul(b[:, i * D:(i + 1) * D], hidden[:, f, i * P:(i + 1) * P],
                                                   w2[:, f, :], start=(f == 0), stop=(f == FC - 1))
                    ins.then_inc(s_job, 1)
                pe.wait_ge(s_ready, c * 3 + 3)
                for n in (0, 1):
                    transpose4(c, J_Q1 + n, lambda i, n=n: normed[:, 4 * n + i, :], J_FFN)
                pe.wait_ge(s_dve_job, c * DVE_JOBS + jobs_read("dve", J_Q1 + 2))
                for h in (0, 1):
                    product(c, J_Q1 + 2 + h, w_t[:, 0, :], normed_t, h, J_FFN)
                all_read(c, J_OUT)
                pe.wait_ge(s_k1st, c * STACKED + STACKED)
                pe.wait_ge(s_bias, c + 1)
                pe.wait_ge(s_qst, c * 2 * STACKED + 2 * STACKED)
                attention(c, U0, U)
                pe.wait_ge(s_probs, c * U + U)
                pe.wait_ge(s_top, c * U + U)
                pe.wait_ge(s_side_read, c * SIDE + SIDE)
                for n in (0, 1):
                    b = open_job(c, J_OUT + n, J_OUT)
                    for i in range(4):
                        ins = nc.tensor.matmul(b[:, i * D:(i + 1) * D],
                                               mix_t[:, (4 * n + i) * P:(4 * n + i + 1) * P], w_t[:, 3, :],
                                               start=True, stop=True)
                    ins.then_inc(s_job, 1)

        @block.vector
        def _(dve):
            steps = [0]

            def step(ins):
                steps[0] += 1
                ins.then_inc(s_step, 1)
                dve.wait_ge(s_step, steps[0])

            dve.wait_ge(s_const, N_CONST)
            step(nc.vector.tensor_copy(cstb[:], cst[:, C_BF:C_BF + CWB]))
            step(nc.vector.tensor_copy(blocks[:], cst[:, C_BL:C_BL + PAIRS].unsqueeze(2).broadcast_to([P, PAIRS, P])))
            dve.wait_ge(s_setup, 9)
            dve.sem_clear(s_step)

            def job(c, n):
                dve.wait_ge(s_job, c * len(JOBS) + n + 1)
                return bank[n % JOB_BANKS]

            def layernorm(c, n, src, dst):
                for t in range(TILES):
                    ins = nc.vector.bn_stats(stat6[:, t, :], src[:, t, :])
                step(ins)
                for t in range(TILES):
                    ins = nc.vector.bn_aggr(mean_var[:, t, :], stat6[:, t, :])
                step(ins)
                nc.vector.tensor_scalar(var_eps[:], mean_var[:, :, 1], EPS, None, ALU.add).then_inc(s_var, 1)
                dve.wait_ge(s_rstd, c * 4 + n + 1)
                for t in range(TILES):
                    ins = nc.vector.tensor_scalar(dst[:, t, :], src[:, t, :], mean_var[:, t, 0:1], rstd[:, t:t + 1],
                                                  ALU.subtract, ALU.mult)
                return ins

            def rows(v, n=TILES):
                return v[:].unsqueeze(1).broadcast_to([P, n, D])

            def scaled(c, n, h, w, b):
                nc.vector.tensor_scalar(normed_t[:, h * HALF:(h + 1) * HALF], job(c, n)[:], cols[:, w:w + 1],
                                        cols[:, b:b + 1], ALU.mult, ALU.add).then_inc(s_dve_job, 1)

            def low(c, hi_count, src, bias, hi, lo):
                dve.wait_ge(s_hi, c * 10 + hi_count)
                return nc.vector.scalar_tensor_tensor(out=lo, in0=src, scalar=bias, in1=hi, op0=ALU.add,
                                                      op1=ALU.subtract)

            def diagonal(c):
                for a in range(PARTS):
                    for s in range(HG):
                        ins = nc.vector.tensor_scalar(
                            q_diag[:, a, :, s, :], q_part[:, a, :].rearrange("p (b q) -> p b q", q=T),
                            hh_mask[:, s:s + 1], None, ALU.mult)
                ins.then_inc(s_diag, 1)

            def take_top(c, u):
                dve.wait_ge(s_scores_q, c * U + u + 1)
                for n in (0, 1):
                    if u < U0:
                        ins = nc.vector.tensor_reduce(top[:, 4 * n:4 * n + 4],
                                                      bank[n][:].rearrange("p (a k) -> p a k", a=4), AX_X, ALU.max,
                                                      negate=True)
                    else:
                        ins = nc.vector.tensor_reduce(top[:, 8 * n:8 * n + 8],
                                                      bank[n][:].rearrange("p (a k) -> p a k", a=8), AX_X, ALU.max,
                                                      negate=True)
                step(ins)
                w = 8 if u < U0 else 16
                nc.vector.tensor_copy(top_rep[:].rearrange("p (r a) -> p r a", a=w),
                                      top[:, 0:w].unsqueeze(1).broadcast_to([P, P // w, w])).then_inc(s_top, 1)

            def make_shift(c, u):
                dve.wait_ge(s_side, c * SIDE + SIDE_AT["top", u] + 1)
                step(nc.vector.tensor_copy(top_hi[:], side[:, 0:P]))
                ins = nc.vector.scalar_tensor_tensor(out=top_row[:], in0=top_hi[:], scalar=lo_row[u >= U0],
                                                     in1=side[:, 0:P], op0=ALU.mult, op1=ALU.add)
                ins.then_inc(s_side_read, 1)
                dve.wait_ge(s_side_read, c * SIDE + SIDE_AT["top", u] + 1)
                if u >= 2:
                    dve.wait_ge(s_scores_k, c * U + u - 1)
                nc.vector.tensor_tensor(shift[u % 2][:], top_row[:].unsqueeze(1).broadcast_to([P, PAIRS, P]),
                                        blocks[:], ALU.mult).then_inc(s_shift, 1)

            def normalize(c, u):
                base = c * SIDE + SIDE_AT["nat", u]
                dve.wait_ge(s_side, base + 1)
                if u < U0:
                    t = u // 2
                    nat = side[:].rearrange("p (s e) -> p s e", s=2)
                    den = [nat[:, s, VW * s + DH:256:32] for s in (0, 1)]
                    for s in (0, 1):
                        ins = nc.vector.reciprocal(rden[:, 8 * s:8 * s + 8], den[s])
                    step(ins)
                    for s in (0, 1):
                        num = nat[:, s].rearrange("p (a w) -> p a w", w=32)[:, :, VW * s:VW * s + DH]
                        ins = nc.vector.tensor_tensor(
                            o_nat[:, 0, 64 * s:64 * s + 64].rearrange("p (a d) -> p a d", d=DH), num,
                            rden[:, 8 * s:8 * s + 8].unsqueeze(2).broadcast_to([P, 8, DH]), ALU.mult)
                    ins.then_inc(s_side_read, 1)
                    dve.wait_ge(s_side_read, base + 1)
                    nc.vector.tensor_tensor(x1[:, t, :], x_in[:, t, :], o_nat[:, 0, :], ALU.add).then_inc(s_x1, 1)
                else:
                    nat = side[:].rearrange("p (h s w) -> p h s w", h=H, s=2)
                    step(nc.vector.reciprocal(rden[:].rearrange("p (h s) -> p h s", s=2), nat[:, :, :, DH]))
                    for s in (0, 1):
                        ins = nc.vector.tensor_tensor(
                            o_nat[:, s, :].rearrange("p (h d) -> p h d", d=DH), nat[:, :, s, 0:DH],
                            rden[:].rearrange("p (h s) -> p h s", s=2)[:, :, s].unsqueeze(2).broadcast_to([P, H, DH]),
                            ALU.mult)
                    ins.then_inc(s_side_read, 1)
                    dve.wait_ge(s_side, base + 2)
                    t = u - U0 - 1
                    nc.vector.tensor_copy(
                        mix_t[:, t * P:(t + 2) * P].rearrange("p (t s q) -> p s t q", t=2, s=2),
                        side[:, 0:256].rearrange("p (s t q) -> p s t q", s=2, t=2)).then_inc(s_side_read, 1)

            def attention(c, first, last):
                take_top(c, first)
                for u in range(first, last):
                    make_shift(c, u)
                    if u + 1 < last:
                        take_top(c, u + 1)
                    if u - 2 > first and u % 2:
                        normalize(c, u - 2)
                normalize(c, last - 1)

            with dve.Fori(0, CHUNKS) as c:
                steps[0] = 0
                dve.wait_ge(s_x, c * 32 + 32)
                dve.wait_ge(s_stored, c * 16)
                layernorm(c, 0, x_in, normed).then_inc(s_ready, 1)
                step(nc.vector.tensor_scalar(keep[:], mask_in[:], 0, None, ALU.not_equal))
                nc.vector.tensor_scalar(
                    k1_stack[ROWS:ROWS + 1], keep[ROWS:ROWS + 1].unsqueeze(1).broadcast_to([1, G, TOK]), -1.0,
                    KEYMASK, ALU.add, ALU.mult).then_inc(s_bias, 1)
                for h in (0, 1):
                    scaled(c, 2 + h, h, G1, BE1)
                dve.wait_ge(s_kst, c * STACKED)
                for s, n, b in ((1, 4, BKC), (0, 6, BK0)):
                    for h in (0, 1):
                        src = job(c, n + h)[:].rearrange("p (b k) -> p b k", k=T)
                        low(c, n - 4 + h + 1, src, cols[:, b:b + 1], k_part[:, 0, 8 * h:8 * h + 8, s, :],
                            k_part[:, 1, 8 * h:8 * h + 8, s, :]).then_inc(s_dve_job, 1)
                dve.wait_ge(s_qst, c * 2 * STACKED)
                for h in (0, 1):
                    low(c, 5 + h, job(c, 8 + h)[:], cols[:, BQ0:BQ0 + 1], q_part[:, 0, h * HALF:(h + 1) * HALF],
                        q_part[:, 1, h * HALF:(h + 1) * HALF]).then_inc(s_dve_job, 1)
                dve.wait_ge(s_dve_job, c * DVE_JOBS + jobs_read("dve", 10))
                diagonal(c)
                for n in range(4):
                    src = job(c, 10 + n)[:].rearrange("p (b s a d) -> p b s a d", b=4, s=2, d=DH)
                    bias = row_bv0[:].rearrange("p (s a d) -> p s a d", s=2, d=DH)
                    for s in (0, 1):
                        ins = nc.vector.tensor_tensor(
                            v0[:, 4 * n:4 * n + 4, :, s, 0:DH], src[:, :, s],
                            bias[:, s].unsqueeze(1).broadcast_to([P, 4, PAIRS, DH]), ALU.add)
                    ins.then_inc(s_dve_job, 1)
                dve.wait_ge(s_k1st, c * STACKED)
                for h in (0, 1):
                    ins = nc.vector.scalar_tensor_tensor(
                        out=k1_full[:, h, :], in0=job(c, 14 + h)[:], scalar=cols[:, BK1:BK1 + 1],
                        in1=keep[:, h * HALF:(h + 1) * HALF], op0=ALU.add, op1=ALU.mult)
                    ins.then_inc(s_dve_job, 1)
                for n in (0, 1):
                    src = job(c, 16 + n)[:].rearrange("p (t h d) -> p t h d", t=4, d=DH)
                    bias = row_bv1[:].rearrange("p (h d) -> p h d", d=DH)
                    for s in (0, 1):
                        r = slice(T * s, T * s + T)
                        ins = nc.vector.tensor_tensor(
                            v1[r, 4 * n:4 * n + 4, :, s, 0:DH], src[r],
                            bias[r].unsqueeze(1).broadcast_to([T, 4, H, DH]), ALU.add)
                    ins.then_inc(s_dve_job, 1)
                for h in (0, 1):
                    at = slice(h * HALF, (h + 1) * HALF)
                    dve.wait_ge(s_hi, c * 10 + 7 + h)
                    ins = nc.vector.tensor_tensor(k1_part[:, 1, at], k1_full[:, h, :], k1_part[:, 0, at], ALU.subtract)
                ins.then_inc(s_k1_lo, 1)
                attention(c, 0, U0)
                dve.wait_ge(s_x1, c * TILES + TILES)
                ins = layernorm(c, 1, x1, normed)
                step(ins)
                step(nc.vector.tensor_tensor(normed[:], normed[:], rows(row_g2), ALU.mult))
                step(nc.vector.tensor_tensor(normed[:], normed[:], rows(row_be2), ALU.add))
                layernorm(c, 2, normed, normed).then_inc(s_ready, 1)
                step(nc.vector.tensor_tensor(x1[:], x1[:], rows(row_b2), ALU.add))
                for h in (0, 1):
                    scaled(c, J_FFN + 6 * h, h, GF, BF)
                    ins = nc.vector.tensor_tensor(
                        x2[:, 4 * h:4 * h + 4, :].rearrange("p t d -> p (t d)"), job(c, J_FFN + 6 * h + 5)[:],
                        x1[:, 4 * h:4 * h + 4, :].rearrange("p t d -> p (t d)"), ALU.add)
                    ins.then_inc(s_dve_job, 1)
                dve.wait_ge(s_dve_job, c * DVE_JOBS + jobs_read("dve", J_Q1))
                layernorm(c, 3, x2, normed).then_inc(s_ready, 1)
                dve.wait_ge(s_ready, c * 3 + 3)
                step(nc.vector.tensor_tensor(x2[:], x2[:], rows(row_bo), ALU.add))
                for h in (0, 1):
                    scaled(c, J_Q1 + h, h, LW, LB)
                for h in (0, 1):
                    low(c, 9 + h, job(c, J_Q1 + 2 + h)[:], cols[:, BQ1:BQ1 + 1],
                        q_part[:, 0, h * HALF:(h + 1) * HALF],
                        q_part[:, 1, h * HALF:(h + 1) * HALF]).then_inc(s_dve_job, 1)
                dve.wait_ge(s_dve_job, c * DVE_JOBS + jobs_read("dve", J_OUT))
                dve.wait_ge(s_qst, c * 2 * STACKED + STACKED)
                diagonal(c)
                attention(c, U0, U)
                for n in (0, 1):
                    ins = nc.vector.tensor_tensor(
                        result[:, 4 * n:4 * n + 4, :].rearrange("p t d -> p (t d)"), job(c, J_OUT + n)[:],
                        x2[:, 4 * n:4 * n + 4, :].rearrange("p t d -> p (t d)"), ALU.add)
                    ins.then_inc(s_dve_job, 1)
                dve.sem_clear(s_step)


_INS = ["x", "ctx_1024", "mask_BxS2_ik0", "L0_xattn_w_qkv", "L0_xattn_b_qkv", "L0_xattn_w_ckv", "L0_xattn_b_ckv",
        "L0_xattn_g1", "L0_xattn_be1", "L0_xattn_g2", "L0_xattn_be2", "L0_xattn_gf", "L0_xattn_bf", "L0_xattn_w1",
        "L0_xattn_b1", "L0_xattn_w2", "L0_xattn_b2", "L1_xattn_ln_w", "L1_xattn_ln_b", "L1_xattn_wq", "L1_xattn_bq",
        "L1_xattn_wk", "L1_xattn_bk", "L1_xattn_wv", "L1_xattn_bv", "L1_xattn_wo", "L1_xattn_bo"]


def kernel(**inputs):
    import numpy as _np
    import concourse.bacc as _bacc
    from concourse import mybir as _mybir
    from concourse.bass_utils import run_bass_kernel_spmd as _run

    nc = _bacc.Bacc("TRN2", target_bir_lowering=False, num_devices=1)
    arrays, io = {}, {}
    for name in _INS + ["constants"]:
        a = _np.ascontiguousarray(constants() if name == "constants" else inputs[name])
        arrays[f"in_{name}"] = a
        io[name] = nc.dram_tensor(f"in_{name}", a.shape, _mybir.dt.from_np(a.dtype), kind="ExternalInput").ap()
    out = nc.dram_tensor("out_0", (B, T, D), F32, kind="ExternalOutput").ap()
    xattn_program(nc, io, io.pop("constants"), out)
    r = _run(nc, [arrays], core_ids=[0])
    return r.results[0]["out_0"]
```

```python
from collections import namedtuple
from contextlib import ExitStack

import concourse.bass as bass
from concourse import mybir

ALU = mybir.AluOpType
ACT = mybir.ActivationFunctionType
AX_X = mybir.AxisListType.X
F32 = mybir.dt.float32
F16 = mybir.dt.float16
BF16 = mybir.dt.bfloat16
I32 = mybir.dt.int32

P = 128
B, T, D = 64, 64, 128
H, DH, F = 16, 8, 512
CB = 8
CHUNKS = B // CB
TOK = CB * T
TILES = TOK // P
FC = F // P
G = 4
HG = H // G
PARTS = 2
TERMS = 3
ROWS = TERMS * HG * DH
Q_PART = (0, 0, 1)
K_PART = (0, 1, 0)
PAIRS = H // 2
VW = 16
TOPS = 32
EPS = 1e-5
SCALE = float(DH) ** -0.5
CAUSAL = -1e30
N_VEC = 12 + FC
KEYMASK = 32768.0
FILL = 16 * TERMS * G

Body = namedtuple("Body", "reg base")
FIRST, LAST = -1, CHUNKS
SLOTS = 12
STARTS = ((FIRST, 8), (0, 8), (LAST, 4))
LAG = {"in": -1, "ffn": 0, "out": 1}


def after(i, n=1):
    return Body(i.reg, i.base + n)


def chunk(stage, i):
    return i.base - LAG[stage] + (0 if i.reg is None else i.reg)


def odd(stage, i):
    return (i.base - LAG[stage]) % 2


def runs(stage, i):
    return i.reg is not None or 0 <= i.base - LAG[stage] < CHUNKS


def unit_stage(t):
    return "ffn" if t < 5 else "out" if t < 9 else "in"


def layer(t):
    return 1 if 5 <= t < 9 else 0


def place(t):
    return t + 3 if t < 5 else t - 5 if t < 9 else t - 9


def ahead(i, t, n):
    for _ in range(n):
        i, t = (after(i), 0) if t == SLOTS - 1 else (i, t + 1)
        if not runs(unit_stage(t), i):
            return None
    return i, t


JOB_LIST = [
    ("ctx_t", 0, "b", "in", 0, "act"), ("k_ctx", 1, "a", "in", 0, "dve"),
    ("x_t", 1, "b", "in", 0, "act"), ("k0", 2, "a", "in", 0, "dve"),
    ("q0", 2, "b", "in", 0, "dve"),
    ("v0a", 3, "a", "in", 0, "dve"), ("v0b", 4, "a", "in", 0, "dve"),
    ("k1", 6, "a", "ffn", 1, "dve"), ("f_t", 7, "b", "ffn", 1, "act"),
    ("w1_0", 8, "b", "ffn", 0, "act"), ("w1_1", 8, "b", "ffn", 1, "act"),
    ("w1_2", 8, "b", "ffn", 0, "act"), ("w1_3", 8, "b", "ffn", 1, "act"),
    ("v1", 9, "a", "ffn", 0, "act"), ("w2", 9, "b", "ffn", 1, "dve"),
    ("out", 11, "a", "out", 0, "dve"), ("x2_t", 11, "a", "ffn", 1, "act"),
    ("q1", 11, "b", "ffn", 1, "dve")]
JOBS = [(name, stage) for name, _, _, stage, _, _ in JOB_LIST]
BANK = {name: bank for name, _, _, _, bank, _ in JOB_LIST}
READER = {name: who for name, _, _, _, _, who in JOB_LIST}
UNITS = [(t, unit_stage(t)) for t in range(SLOTS)]
NORMS = [("x", "in"), ("x1", "ffn"), ("x1_again", "ffn"), ("x2", "ffn")]
HIGHS = [("k_ctx", "in"), ("k0", "in"), ("q0", "in"), ("k1", "ffn"), ("q1", "ffn")]
DIAGS = [("q1", "out"), ("q0_hi", "in"), ("q0", "in"), ("q1_hi", "ffn")]
NAT = {1: "ffn", 3: "ffn", 5: "ffn", 7: "out", 9: "out", 11: "in"}
BACK = (8, 10)
RESIDUALS = [(t, NAT[t]) for t in (1, 3, 5, 11)]
POOLED = [("keep", "ffn"), ("mask_row", "ffn"), ("gain", "ffn"), ("offset", "ffn"), ("x1_b2", "ffn"),
          ("x2_bo", "ffn")]
SIDES = []
for _t in range(SLOTS):
    if _t in NAT:
        SIDES.append((("nat", _t), NAT[_t]))
    if _t in BACK:
        SIDES.append((("back", _t), "out"))


def happens(name, stage, b):
    return runs(stage, Body(None, b))


def nth(events, i, name, who=None):
    names = [e[0] for e in events]

    def upto(b):
        whole = sum(happens(n, s, a) for a in range(FIRST, b) for n, s in events if who in (None, READER.get(n)))
        part = [e for e in events[:names.index(name) + 1] if who in (None, READER.get(e[0]))]
        return whole + sum(happens(n, s, b) for n, s in part if b >= FIRST)

    n = upto(i.base)
    if i.reg is None:
        return n
    period = len([e for e in events if who in (None, READER.get(e[0]))])
    assert n > 0 and upto(i.base + 1) - n == period
    return i.reg * period + n


def some(count):
    return not isinstance(count, int) or count > 0


def job_before(i, name):
    same = [n for n, _ in JOBS if BANK[n] == BANK[name]]
    n = same.index(name)
    if n:
        return i, same[n - 1]
    return after(i, -1), [m for m, _ in JOBS if READER[m] == READER[same[-1]]][-1]


C_ID, C_HH = 0, P
CW = P + HG
C_IDB, C_EQ, C_HK, C_HQ = 0, P, 2 * P, 2 * P + T
CWB = C_HQ + 2 * T
C_S0 = 0
C_S1 = PAIRS * P
CWS = 2 * PAIRS * P


def constants():
    import numpy as np

    p = np.arange(P)[:, None]
    c = np.arange(P)[None, :]
    k = np.arange(T)[None, :]
    out = np.zeros((P, CW + CWB + CWS), np.float32)
    out[:, C_ID:C_ID + P] = p == c
    out[:, C_HH:C_HH + HG] = p % (HG * DH) // DH == np.arange(HG)
    b = out[:, CW:CW + CWB]
    b[:, C_IDB:C_IDB + P] = p == c
    b[:, C_EQ:C_EQ + P] = (p == c % T) & (p < T)
    b[:, C_HK:C_HK + T] = np.where((k > p) & (p < T), CAUSAL, 0.0)
    b[:, C_HQ:C_HQ + 2 * T] = np.where((p - T > c % T), CAUSAL, 0.0)
    s = out[:, CW + CWB:]
    for a in range(PAIRS):
        s[:, C_S0 + P * a:C_S0 + P * a + P] = ((p < 16) & (p % PAIRS == a)) | (p - T == c)
        s[:, C_S1 + P * a:C_S1 + P * a + P] = (p < TOPS) & (p % PAIRS == a) & (p // PAIRS % 2 == c // T)
    return out


def xattn_program(nc, io, consts, out):
    ctx = ExitStack()
    with ctx:
        def sb(name, shape, dt=F32):
            return ctx.enter_context(nc.sbuf_tensor(name, shape, dt))

        def two(name, shape, dt=F32):
            return [sb(f"{name}{n}", shape, dt) for n in (0, 1)]

        def sem(name):
            return ctx.enter_context(nc.semaphore(name))

        w_qkv = sb("w_qkv", [P, 3 * D])
        w_ckv = sb("w_ckv", [P, 2 * D])
        w1 = sb("w1", [P, F])
        w2 = sb("w2", [P, FC, D])
        w_t = sb("w_t", [P, 4, D])
        vectors = sb("vectors", [N_VEC, P])
        cols = sb("cols", [P, N_VEC])
        (G1, BE1, GF, BF, LW, LB, BQ0, BK0, BKC, BQ1, BK1, BV1) = range(12)
        B1 = 12
        row_g2 = sb("row_g2", [P, D])
        row_be2 = sb("row_be2", [P, D])
        row_b2 = sb("row_b2", [P, D])
        row_bv0 = sb("row_bv0", [P, D])
        row_bo = sb("row_bo", [P, D])
        half = sb("half", [P, TILES])
        cst = sb("cst", [P, CW + CWB])
        cstb = sb("cstb", [P, CWB], BF16)
        spread = sb("spread", [P, CWS], BF16)
        identity = cst[:, C_ID:C_ID + P]
        hh_mask = cst[:, C_HH:C_HH + HG]
        identity_b = cstb[:, C_IDB:C_IDB + P]
        eye_query = cstb[:, C_EQ:C_EQ + P]
        hide_key = cstb[:, C_HK:C_HK + T]

        x_in = two("x_in", [P, TILES, D])
        ctx_in = sb("ctx_in", [P, TILES, D])
        normed = sb("normed", [P, TILES, D])
        normed_t = sb("normed_t", [P, TOK])
        normed_f = sb("normed_f", [P, TILES, D])
        normed_ft = sb("normed_ft", [P, TOK])
        ctx_t = two("ctx_t", [P, TOK])
        q_part = sb("q_part", [P, PARTS, TOK], F16)
        q_diag = sb("q_diag", [P, PARTS, CB, HG, T], F16)
        k_part = sb("k_part", [P, PARTS, CB, 2, T], F16)
        k1_part = sb("k1_part", [P, PARTS, TOK], F16)
        q_stack = two("q_stack", [P, G, CB, HG * T], F16)
        k_stack = two("k_stack", [P, G, CB, 2 * T], F16)
        q1_stack = sb("q1_stack", [P, G, CB, HG * T], F16)
        k1_stack = sb("k1_stack", [P, G, TOK], F16)
        v0 = two("v0", [P, CB, H, VW])
        v1 = sb("v1", [P, TILES, H, 2, VW])
        probs = two("probs", [P, H, T])
        top = two("top", [P, 2, PAIRS])
        top_rep = [sb(f"top_rep{n}", [P, TOPS], BF16) for n in range(3)]
        top_row = two("top_row", [P, P], BF16)
        stat6 = sb("stat6", [P, TILES, 6])
        mean_var = {n: sb(f"mean_var_{n}", [P, TILES, 2]) for n, _ in NORMS}
        var_eps = {n: sb(f"var_eps_{n}", [P, TILES]) for n, _ in NORMS}
        rstd = {n: sb(f"rstd_{n}", [P, TILES]) for n, _ in NORMS}
        o_t = sb("o_t", [P, 4, 2, T])
        rden = sb("rden", [P, 32])
        o_nat = sb("o_nat", [P, 2, D])
        x1 = two("x1", [P, TILES, D])
        x2 = two("x2", [P, TILES, D])
        hidden = sb("hidden", [P, FC, TOK])
        k1_full = sb("k1_full", [P, TOK])
        mix_t = sb("mix_t", [P, TOK])
        mask_in = sb("mask_in", [P, TOK], I32)
        keep = sb("keep", [P, TOK])
        mask_row = two("mask_row", [P, TOK], F16)
        result = sb("result", [P, TILES, D])
        w_nat = k1_full
        spread_in = hidden

        bank = [ctx.enter_context(nc.psum_tensor(f"bank{n}", [P, 512], F32)) for n in range(8)]
        query_bank, key_bank, dense_bank, side, mixed = bank[0:2], bank[2:4], bank[4:6], bank[6], bank[7]
        turned = mixed[0:TOPS, 256:256 + P // 2].bitcast(BF16)

        s_const = sem("s_const")
        s_late = sem("s_late")
        s_cols = sem("s_cols")
        s_cols_read = sem("s_cols_read")
        s_wt = sem("s_wt")
        s_wt_read = sem("s_wt_read")
        s_setup = sem("s_setup")
        s_cast = sem("s_cast")
        s_x = sem("s_x")
        s_ctx = sem("s_ctx")
        s_mask = sem("s_mask")
        s_taken = sem("s_taken")
        s_var = sem("s_var")
        s_rstd = sem("s_rstd")
        s_norm = sem("s_norm")
        s_job = sem("s_job")
        s_act_job = sem("s_act_job")
        s_dve_job = sem("s_dve_job")
        s_hi = sem("s_hi")
        s_diag = sem("s_diag")
        s_k1_lo = sem("s_k1_lo")
        s_kst = sem("s_kst")
        s_qst = sem("s_qst")
        s_k1st = sem("s_k1st")
        s_q1st = sem("s_q1st")
        s_pool = sem("s_pool")
        s_scores_q = sem("s_scores_q")
        s_top = sem("s_top")
        s_turned = sem("s_turned")
        s_row = sem("s_row")
        s_scores_k = sem("s_scores_k")
        s_probs = sem("s_probs")
        s_mixed = sem("s_mixed")
        s_o_t = sem("s_o_t")
        s_side = sem("s_side")
        s_side_read = sem("s_side_read")
        s_x1 = sem("s_x1")
        s_stored = sem("s_stored")
        s_step = sem("s_step")

        tokens = lambda a: a.rearrange("(c t b) q d -> c (b q) t d", c=CHUNKS, b=2)
        x_d, ctx_d, out_d = tokens(io["x"]), tokens(io["ctx_1024"]), tokens(out)
        mask_d = io["mask_BxS2_ik0"].rearrange("(c b) k -> c (b k)", c=CHUNKS)
        block = ctx.enter_context(nc.Block())

        def across(v):
            return v.partition_broadcast(P)

        col_of = [("L0_xattn_g1", 0), ("L0_xattn_be1", 0), ("L0_xattn_gf", 0), ("L0_xattn_bf", 0),
                  ("L1_xattn_ln_w", 0), ("L1_xattn_ln_b", 0), ("L0_xattn_b_qkv", 0),
                  ("L0_xattn_b_qkv", D), ("L0_xattn_b_ckv", 0), ("L1_xattn_bq", 0),
                  ("L1_xattn_bk", 0), ("L1_xattn_bv", 0)]
        first_loads = [(cst[:], consts[:, 0:CW + CWB])]
        first_loads += [(vectors[n:n + 1, :], io[v][o:o + D].rearrange("(a p) -> a p", a=1))
                        for n, (v, o) in enumerate(col_of)]
        first_loads += [(vectors[B1:B1 + FC, :], io["L0_xattn_b1"].rearrange("(c p) -> c p", p=P)),
                        (w_ckv[:], io["L0_xattn_w_ckv"]), (w_qkv[:], io["L0_xattn_w_qkv"]),
                        (row_bv0[0:T], io["L0_xattn_b_qkv"][2 * D:3 * D].partition_broadcast(T)),
                        (row_bv0[T:P], io["L0_xattn_b_ckv"][D:2 * D].partition_broadcast(T))]
        late_loads = [(spread_in[:].rearrange("p a b -> p (a b)"), consts[:, CW + CWB:CW + CWB + CWS])]
        late_loads += [(w_nat[:, n * D:(n + 1) * D], io[f"L1_xattn_{w}"])
                       for n, w in enumerate(("wq", "wk", "wv", "wo"))]
        late_loads += [(w1[:], io["L0_xattn_w1"]), (w2[:], io["L0_xattn_w2"].rearrange("(c p) n -> p c n", p=P)),
                       (row_g2[:], across(io["L0_xattn_g2"])), (row_be2[:], across(io["L0_xattn_be2"])),
                       (row_b2[:], across(io["L0_xattn_b2"])), (row_bo[:], across(io["L1_xattn_bo"]))]
        N_CONST, N_LATE = 16 * len(first_loads), 16 * len(late_loads)

        def pipeline(engine, body):
            body(Body(None, -1))
            body(Body(None, 0))
            with engine.Fori(0, CHUNKS - 3, 2) as r:
                body(Body(r, 1))
                body(Body(r, 2))
            body(Body(None, CHUNKS - 1))
            body(Body(None, CHUNKS))

        @block.sync
        def _(sp):
            def fill(stack, part, order, filled, terms=range(TERMS)):
                for t in terms:
                    for g in range(G):
                        rows = slice(HG * DH * g, HG * DH * (g + 1))
                        sp.dma_start(stack[HG * DH * t:HG * DH * (t + 1), g], part[rows, order[t]]).then_inc(filled, 16)

            def body(i):
                diag = q_diag[:].rearrange("p a b h q -> p a b (h q)")
                if runs("in", i):
                    c = chunk("in", i)
                    n_before = nth(RESIDUALS, after(i, -1), 5)
                    if some(n_before):
                        sp.wait_ge(s_x1, n_before)
                    sp.dma_start(x_in[odd("in", i)][:], x_d[c]).then_inc(s_x, 16)
                    if i.base != FIRST:
                        sp.wait_ge(s_act_job, nth(JOBS, after(i, -1), "ctx_t", "act"))
                    sp.dma_start(ctx_in[:], ctx_d[c]).then_inc(s_ctx, 16)
                if i.base == FIRST:
                    for dst, src in first_loads:
                        sp.dma_start(dst, src).then_inc(s_const, 16)
                if runs("ffn", i):
                    n_before = nth(POOLED, after(i, -1), "mask_row")
                    if some(n_before):
                        sp.wait_ge(s_pool, n_before)
                    sp.dma_start(mask_in[:], mask_d[chunk("ffn", i)].partition_broadcast(P)).then_inc(s_mask, 16)
                if runs("out", i):
                    sp.wait_ge(s_diag, nth(DIAGS, after(i, -1), "q1_hi"))
                    fill(q1_stack, diag, Q_PART, s_q1st, (0, 1))
                    sp.wait_ge(s_diag, nth(DIAGS, i, "q1"))
                    fill(q1_stack, diag, Q_PART, s_q1st, (2,))
                if runs("in", i):
                    sp.wait_ge(s_dve_job, nth(JOBS, i, "k0", "dve"))
                    fill(k_stack[odd("in", i)], k_part[:].rearrange("p a b s k -> p a b (s k)"), K_PART, s_kst)
                    sp.wait_ge(s_diag, nth(DIAGS, i, "q0_hi"))
                    fill(q_stack[odd("in", i)], diag, Q_PART, s_qst, (0, 1))
                    sp.wait_ge(s_diag, nth(DIAGS, i, "q0"))
                    fill(q_stack[odd("in", i)], diag, Q_PART, s_qst, (2,))
                if runs("ffn", i):
                    sp.wait_ge(s_k1_lo, chunk("ffn", i) + 1)
                    fill(k1_stack, k1_part, K_PART, s_k1st)
                    sp.dma_start(k1_stack[ROWS:ROWS + 1], mask_row[odd("ffn", i)][ROWS:ROWS + 1].unsqueeze(1).broadcast_to(
                        [1, G, TOK])).then_inc(s_k1st, 16)
                if runs("out", i):
                    sp.wait_ge(s_dve_job, nth(JOBS, i, "out", "dve"))
                    sp.dma_start(out_d[chunk("out", i)], result[:]).then_inc(s_stored, 16)

            pipeline(sp, body)
            sp.wait_ge(s_stored, 16 * (CHUNKS + 1))

        @block.gpsimd
        def _(pool):
            fills = [(half[:], -0.5), (v0[0][:], 0.0), (v0[1][:], 0.0), (top_row[0][:], 0.0), (top_row[1][:], 0.0),
                     (top_rep[0][:], 0.0), (top_rep[1][:], 0.0), (top_rep[2][:], 0.0)]
            fills += [(v0[n][:, :, :, DH:DH + 1], 1.0) for n in (0, 1)]
            fills += [(v1[:], 0.0), (v1[0:T, :, :, 0, DH:DH + 1], 1.0), (v1[T:P, :, :, 1, DH:DH + 1], 1.0),
                      (k1_stack[ROWS:P], 0.0), (q1_stack[ROWS:P], 0.0), (q1_stack[ROWS:ROWS + 1], KEYMASK)]

            def set_up():
                nc.gpsimd.memset(keep[:], 0.0).then_inc(s_stored, 16)
                pool.wait_ge(s_stored, 16)
                for n, (dst, value) in enumerate(fills):
                    nc.gpsimd.memset(dst, value).then_inc(s_setup, 1)
                    pool.wait_ge(s_setup, n + 1)

            def root(i, name):
                pool.wait_ge(s_var, nth(NORMS, i, name))
                nc.gpsimd.tensor_tensor(rstd[name][:], var_eps[name][:], half[:], ALU.pow).then_inc(s_rstd, 1)

            def rows(v):
                return v[:].unsqueeze(1).broadcast_to([P, TILES, D])

            def body(i):
                if i.base == FIRST:
                    for dst, src in late_loads:
                        nc.gpsimd.dma_start(dst, src).then_inc(s_late, 16)
                    set_up()
                if runs("ffn", i):
                    pool.wait_ge(s_mask, 16 * (chunk("ffn", i) + 1))
                    pool.wait_ge(s_dve_job, nth(JOBS, after(i, -1), "q1", "dve"))
                if runs("in", i):
                    root(i, "x")
                if i.base == 0:
                    pool.wait_ge(s_late, N_LATE)
                if runs("ffn", i):
                    o = odd("ffn", i)
                    nc.gpsimd.tensor_scalar(keep[:], mask_in[:], 0, 0, ALU.is_equal, ALU.is_equal).then_inc(s_pool, 1)
                    nc.gpsimd.tensor_scalar(mask_row[o][:], mask_in[:], 0, -KEYMASK, ALU.is_equal,
                                            ALU.mult).then_inc(s_pool, 1)
                    root(i, "x1")
                    pool.wait_ge(s_norm, nth(NORMS, i, "x1"))
                    nc.gpsimd.tensor_tensor(normed_f[:], normed_f[:], rows(row_g2), ALU.mult).then_inc(s_pool, 1)
                    pool.wait_ge(s_pool, nth(POOLED, i, "gain"))
                    nc.gpsimd.tensor_tensor(normed_f[:], normed_f[:], rows(row_be2), ALU.add).then_inc(s_pool, 1)
                    root(i, "x1_again")
                    nc.gpsimd.tensor_tensor(x1[o][:], x1[o][:], rows(row_b2), ALU.add).then_inc(s_pool, 1)
                    root(i, "x2")
                    pool.wait_ge(s_norm, nth(NORMS, i, "x2"))
                    nc.gpsimd.tensor_tensor(x2[o][:], x2[o][:], rows(row_bo), ALU.add).then_inc(s_pool, 1)

            pipeline(pool, body)

        N_FILLS = 16

        @block.scalar
        def _(act):
            def job(i, name):
                act.wait_ge(s_job, nth(JOBS, i, name))
                return dense_bank[BANK[name]]

            def exp(i, t):
                for n in (0, 1):
                    act.wait_ge(s_scores_k, 2 * nth(UNITS, i, t) - 1 + n)
                    nc.scalar.activation(
                        probs[t % 2][:, 8 * n:8 * n + 8].rearrange("p h q -> p (h q)"), key_bank[n][:],
                        ACT.Exp, scale=SCALE).then_inc(s_probs, 1)

            def copy_rows(i, t):
                act.wait_ge(s_turned, nth(UNITS, i, t))
                nc.scalar.copy(top_row[t % 2][0:TOPS], turned).then_inc(s_row, 1)

            def copy_mixed(i, t):
                act.wait_ge(s_mixed, nth(UNITS, i, t))
                if ahead(i, t, 2):
                    act.wait_ge(s_turned, nth(UNITS, *ahead(i, t, 2)))
                if t % 2:
                    act.wait_ge(s_side, nth(SIDES, i, ("nat", t)))
                half_of = (t + 1) % 2
                if layer(t) == 0:
                    dst = o_t[:, :, half_of, :].rearrange("p (s a) q -> p a s q", s=2)
                    src = mixed[:, 0:256].rearrange("p (a s q) -> p a s q", a=2, s=2)
                else:
                    dst = o_t[:, :, half_of, :]
                    src = mixed[:, 0:256].rearrange("p (g q) -> p g q", g=G)
                nc.scalar.copy(dst, src).then_inc(s_o_t, 1)

            def mix(i, t):
                act.wait_ge(s_side, nth(SIDES, i, ("back", t)))
                if i.base > 0:
                    act.wait_ge(s_job, nth(JOBS, after(i, -1), "q1"))
                at = 2 * P * BACK.index(t)
                nc.scalar.activation(
                    mix_t[:, at:at + 2 * P].rearrange("p (t s q) -> p s t q", t=2, s=2),
                    side[:, 0:2 * P].rearrange("p (s t q) -> p s t q", s=2, t=2), ACT.Identity,
                    bias=cols[:, BV1:BV1 + 1]).then_inc(s_side_read, 1)

            def high(i, name, dst, src, bias):
                nc.scalar.activation(dst, src, ACT.Identity, bias=cols[:, bias:bias + 1]).then_inc(s_hi, 1)

            def keys(name, i):
                return job(i, name)[:].rearrange("p (b k) -> p b k", k=T)

            def scaled(i, name, dst, gain, offset):
                nc.scalar.activation(dst[:], job(i, name)[:], ACT.Identity, scale=cols[:, gain:gain + 1],
                                     bias=cols[:, offset:offset + 1]).then_inc(s_act_job, 1)

            def dense(i, t, where):
                if (t, where) == (0, "b") and runs("in", i):
                    nc.scalar.copy(ctx_t[odd("in", i)][:], job(i, "ctx_t")[:]).then_inc(s_act_job, 1)
                if (t, where) == (1, "a") and runs("in", i):
                    if i.base > FIRST:
                        act.wait_ge(s_kst, FILL * chunk("in", i))
                    high(i, "k_ctx", k_part[:, 0, :, 1, :], keys("k_ctx", i), BKC)
                if (t, where) == (1, "b") and runs("in", i):
                    scaled(i, "x_t", normed_t, G1, BE1)
                if (t, where) == (2, "a") and runs("in", i):
                    high(i, "k0", k_part[:, 0, :, 0, :], keys("k0", i), BK0)
                if (t, where) == (2, "b") and runs("in", i):
                    n_before = nth(DIAGS, i, "q1")
                    if some(n_before):
                        act.wait_ge(s_diag, n_before)
                    high(i, "q0", q_part[:, 0], job(i, "q0")[:], BQ0)
                if (t, where) == (6, "a") and runs("ffn", i):
                    act.wait_ge(s_dve_job, nth(JOBS, i, "k1", "dve"))
                    if i.base > 0:
                        act.wait_ge(s_k1st, (FILL + 16) * chunk("ffn", i))
                    nc.scalar.copy(k1_part[:, 0], k1_full[:]).then_inc(s_hi, 1)
                if (t, where) == (7, "b") and runs("ffn", i):
                    scaled(i, "f_t", normed_ft, GF, BF)
                if (t, where) == (8, "b") and runs("ffn", i):
                    if i.base > 0:
                        act.wait_ge(s_job, nth(JOBS, after(i, -1), "q1"))
                    for f in range(FC):
                        nc.scalar.activation(hidden[:, f, :], job(i, f"w1_{f}")[:], ACT.Gelu,
                                             bias=cols[:, B1 + f:B1 + f + 1]).then_inc(s_act_job, 1)
                if (t, where) == (9, "a") and runs("ffn", i):
                    src = job(i, "v1")[:].rearrange("p (t h d) -> p t h d", t=TILES, d=DH)
                    for s in (0, 1):
                        r = slice(T * s, T * s + T)
                        ins = nc.scalar.copy(v1[r, :, :, s, 0:DH], src[r])
                    ins.then_inc(s_act_job, 1)
                if (t, where) == (11, "a") and runs("ffn", i):
                    scaled(i, "x2_t", normed_ft, LW, LB)
                if (t, where) == (11, "b") and runs("ffn", i):
                    act.wait_ge(s_diag, nth(DIAGS, i, "q0"))
                    high(i, "q1", q_part[:, 0], job(i, "q1")[:], BQ1)

            def body(i):
                for t in range(SLOTS):
                    unit = runs(unit_stage(t), i)
                    start = (i.base, t) in STARTS
                    if start:
                        copy_rows(i, t + 1)
                    if t in BACK and runs("out", i):
                        mix(i, t)
                    dense(i, t, "a")
                    if (unit or start) and ahead(i, t, 1):
                        exp(*ahead(i, t, 1))
                    if unit:
                        copy_mixed(i, t)
                    if (unit or start) and ahead(i, t, 2):
                        copy_rows(*ahead(i, t, 2))
                    dense(i, t, "b")
                    if (i.base, t) == (FIRST, 11):
                        act.wait_ge(s_wt, 1)
                        nc.scalar.copy(w_t[:].rearrange("p w n -> p (w n)"), dense_bank[1][:]).then_inc(s_wt_read, 1)

            act.wait_ge(s_cols, 1)
            nc.scalar.copy(cols[:], query_bank[1][:, 0:N_VEC]).then_inc(s_cols_read, 1)
            act.wait_ge(s_cols_read, 1)
            act.wait_ge(s_setup, N_FILLS)
            pipeline(act, body)

        @block.tensor
        def _(pe):
            pe.wait_ge(s_const, N_CONST)
            nc.tensor.transpose(query_bank[1][:, 0:N_VEC], vectors[:], cst[0:N_VEC, C_ID:C_ID + N_VEC]).then_inc(
                s_cols, 1)
            pe.wait_ge(s_cols_read, 1)

            def open_job(i, name):
                before, other = job_before(i, name)
                if before.base >= FIRST:
                    who = READER[other]
                    pe.wait_ge(s_act_job if who == "act" else s_dve_job, nth(JOBS, before, other, who))
                return dense_bank[BANK[name]]

            def transposes(i, name, src):
                b = open_job(i, name)
                for n in range(TILES):
                    ins = nc.tensor.transpose(b[:, n * P:(n + 1) * P], src[:, n, :], identity)
                ins.then_inc(s_job, 1)

            def product(i, name, w, src):
                b = open_job(i, name)
                nc.tensor.matmul(b[:], w, src[:], start=True, stop=True).then_inc(s_job, 1)

            def by_tokens(i, name, src_t, w):
                b = open_job(i, name)
                for n in range(TILES):
                    ins = nc.tensor.matmul(b[:, n * D:(n + 1) * D], src_t[:, n * P:(n + 1) * P], w, start=True,
                                           stop=True)
                ins.then_inc(s_job, 1)

            def dense(i, t, where):
                o = odd("in", i)
                if (t, where) == (0, "b") and runs("in", i):
                    pe.wait_ge(s_ctx, 16 * (chunk("in", i) + 1))
                    transposes(i, "ctx_t", ctx_in)
                if (t, where) == (1, "a") and runs("in", i):
                    pe.wait_ge(s_act_job, nth(JOBS, i, "ctx_t", "act"))
                    product(i, "k_ctx", w_ckv[:, 0:D], ctx_t[o])
                if (t, where) == (1, "b") and runs("in", i):
                    pe.wait_ge(s_norm, nth(NORMS, i, "x"))
                    transposes(i, "x_t", normed)
                if (t, where) == (2, "a") and runs("in", i):
                    pe.wait_ge(s_act_job, nth(JOBS, i, "x_t", "act"))
                    product(i, "k0", w_qkv[:, D:2 * D], normed_t)
                if (t, where) == (2, "b") and runs("in", i):
                    product(i, "q0", w_qkv[:, 0:D], normed_t)
                if t in (3, 4) and where == "a" and runs("in", i):
                    name = ("v0a", "v0b")[t - 3]
                    b = open_job(i, name)
                    for n in range(4):
                        at = slice((4 * (t - 3) + n) * T, (4 * (t - 3) + n + 1) * T)
                        nc.tensor.matmul(b[0:T, n * D:(n + 1) * D], normed_t[:, at], w_qkv[:, 2 * D:3 * D],
                                         start=True, stop=True)
                        ins = nc.tensor.matmul(b[T:P, n * D:(n + 1) * D], ctx_t[o][:, at], w_ckv[:, D:2 * D],
                                               start=True, stop=True)
                    ins.then_inc(s_job, 1)
                if (t, where) == (6, "a") and runs("ffn", i):
                    product(i, "k1", w_t[:, 1, :], ctx_t[odd("ffn", i)])
                if (t, where) == (7, "b") and runs("ffn", i):
                    pe.wait_ge(s_norm, nth(NORMS, i, "x1_again"))
                    transposes(i, "f_t", normed_f)
                if (t, where) == (8, "b") and runs("ffn", i):
                    pe.wait_ge(s_act_job, nth(JOBS, i, "f_t", "act"))
                    for f in range(FC):
                        product(i, f"w1_{f}", w1[:, f * P:(f + 1) * P], normed_ft)
                if (t, where) == (9, "a") and runs("ffn", i):
                    by_tokens(i, "v1", ctx_t[odd("ffn", i)], w_t[:, 2, :])
                if (t, where) == (9, "b") and runs("ffn", i):
                    b = open_job(i, "w2")
                    for n in range(TILES):
                        for f in range(FC):
                            ins = nc.tensor.matmul(b[:, n * D:(n + 1) * D], hidden[:, f, n * P:(n + 1) * P],
                                                   w2[:, f, :], start=(f == 0), stop=(f == FC - 1))
                    ins.then_inc(s_job, 1)
                if (t, where) == (11, "a") and runs("out", i):
                    pe.wait_ge(s_side_read, nth(SIDES, i, ("back", 10)))
                    by_tokens(i, "out", mix_t, w_t[:, 3, :])
                if (t, where) == (11, "a") and runs("ffn", i):
                    pe.wait_ge(s_norm, nth(NORMS, i, "x2"))
                    transposes(i, "x2_t", normed_f)
                if (t, where) == (11, "b") and runs("ffn", i):
                    pe.wait_ge(s_act_job, nth(JOBS, i, "x2_t", "act"))
                    product(i, "q1", w_t[:, 0, :], normed_ft)

            def by_query(i, t):
                c, b, o = chunk(unit_stage(t), i), place(t), odd(unit_stage(t), i)
                if t in (5, 9):
                    pe.wait_ge(s_kst if t == 9 else s_k1st, (FILL if t == 9 else FILL + 16) * (c + 1))
                    pe.wait_ge(s_qst if t == 9 else s_q1st, FILL * (c + 1))
                for n in (0, 1):
                    n_before = 2 * (nth(UNITS, i, t) - 1) - 1 + n
                    if some(n_before):
                        pe.wait_ge(s_taken, n_before)
                    if layer(t) == 0:
                        nc.tensor.matmul(
                            query_bank[n][:].rearrange("p (a k) -> p a k", a=4)[:, :, 0:T], eye_query,
                            hide_key.unsqueeze(1).broadcast_to([P, 4, T]), start=True, stop=False,
                            skip_group_check=True)
                        for a in range(4):
                            g, half_of = 2 * n + a // 2, a % 2
                            ins = nc.tensor.matmul(
                                query_bank[n][:, a * P:(a + 1) * P],
                                q_stack[o][0:ROWS, g, b, P * half_of:P * half_of + P],
                                k_stack[o][0:ROWS, g, b, :], start=False, stop=(a == 3),
                                skip_group_check=True)
                    else:
                        s = 2 * b + n
                        for a in range(PAIRS):
                            ins = nc.tensor.matmul(
                                query_bank[n][:, a * T:(a + 1) * T],
                                q1_stack[:, a // 2, s, P * (a % 2):P * (a % 2) + P],
                                k1_stack[:, a // 2, s * T:(s + 1) * T], start=(a == 0), stop=(a == PAIRS - 1),
                                skip_group_check=True)
                    ins.then_inc(s_scores_q, 1)

            def by_key(i, t, n):
                b, o = place(t), odd(unit_stage(t), i)
                n_before = 2 * nth(UNITS, i, t) - 3 + n
                if some(n_before):
                    pe.wait_ge(s_probs, n_before)
                for m in (0, 1):
                    if layer(t) == 0:
                        nc.tensor.matmul(key_bank[n][:, 256 * m:256 * m + 256], k_stack[o][0:ROWS, 2 * n + m, b, :],
                                         q_stack[o][0:ROWS, 2 * n + m, b, :], start=(m == 0), stop=False,
                                         skip_group_check=True)
                    else:
                        for s in (0, 1):
                            at = 2 * b + s
                            nc.tensor.matmul(
                                key_bank[n][T * s:T * s + T, 256 * m:256 * m + 256],
                                k1_stack[:, 2 * n + m, at * T:(at + 1) * T], q1_stack[:, 2 * n + m, at, :],
                                start=(m == 0), stop=False, skip_group_check=True)
                pe.wait_ge(s_row, nth(UNITS, i, t))
                to_keys = C_S1 if layer(t) else C_S0
                for a in range(4 * n, 4 * n + 4):
                    ins = nc.tensor.matmul(key_bank[n][:, P * (a % 4):P * (a % 4) + P],
                                           spread[:, to_keys + P * a:to_keys + P * a + P], top_row[t % 2][:],
                                           start=False, stop=(a % 4 == 3), skip_group_check=True)
                ins.then_inc(s_scores_k, 1)

            def top_to_rows(i, t):
                pe.wait_ge(s_top, nth(UNITS, i, t))
                n_before = nth(UNITS, i, t) - 1
                if some(n_before):
                    pe.wait_ge(s_row, n_before)
                nc.tensor.transpose(turned, top_rep[t % 3][:], identity_b).then_inc(s_turned, 1)

            def to_tokens(i, t):
                pe.wait_ge(s_o_t, nth(UNITS, i, t) - 1 if runs(unit_stage(t), i) else nth(UNITS, i, t))
                n_before = nth(SIDES, i, ("nat", t)) - 1
                if some(n_before):
                    pe.wait_ge(s_side_read, n_before)
                for n in range(4):
                    ins = nc.tensor.transpose(side[:, n * P:(n + 1) * P], o_t[:, n].rearrange("p b q -> p (b q)"),
                                              identity)
                ins.then_inc(s_side, 1)

            def to_features(i, t):
                n_before = nth(SIDES, i, ("back", t)) - 1
                if some(n_before):
                    pe.wait_ge(s_side_read, n_before)
                for s in (0, 1):
                    ins = nc.tensor.transpose(side[:, s * P:(s + 1) * P], o_nat[:, s, :], identity)
                ins.then_inc(s_side, 1)

            def values(i, t, n):
                pe.wait_ge(s_probs, 2 * nth(UNITS, i, t) - 1 + n)
                if n == 0:
                    n_before = nth(UNITS, i, t) - 1
                    if some(n_before):
                        pe.wait_ge(s_o_t, n_before)
                    if ahead(i, t, 1):
                        pe.wait_ge(s_row, nth(UNITS, *ahead(i, t, 1)))
                pr, b = probs[t % 2], place(t)
                if layer(t) == 0:
                    for p in range(4 * n, 4 * n + 4):
                        j, a = p % 4, p // 4
                        ins = nc.tensor.matmul(
                            mixed[32 * j:32 * j + 32, P * a:P * a + P],
                            v0[odd(unit_stage(t), i)][:, b, 2 * p:2 * p + 2].rearrange("p s w -> p (s w)"),
                            pr[:, 2 * p:2 * p + 2].rearrange("p s q -> p (s q)"), start=True, stop=True)
                else:
                    for h in range(8 * n, 8 * n + 8):
                        j, g = h % 4, h // 4
                        ins = nc.tensor.matmul(
                            mixed[32 * j:32 * j + 32, T * g:T * g + T],
                            v1[:, b, h].rearrange("p s w -> p (s w)"), pr[:, h, :], start=True, stop=True)
                if n == 1:
                    ins.then_inc(s_mixed, 1)

            def body(i):
                for t in range(SLOTS):
                    unit = runs(unit_stage(t), i)
                    if (i.base, t) == (FIRST, 8):
                        pe.wait_ge(s_cast, 4)
                        pe.wait_ge(s_setup, N_FILLS)
                        pe.wait_ge(s_late, N_LATE)
                    start = (i.base, t) in STARTS
                    if start:
                        by_query(i, t + 1)
                        by_query(i, t + 2)
                        top_to_rows(i, t + 1)
                    if t in NAT and runs(NAT[t], i):
                        to_tokens(i, t)
                    if t in BACK and runs("out", i):
                        to_features(i, t)
                    dense(i, t, "a")
                    if (unit or start) and ahead(i, t, 3):
                        by_query(*ahead(i, t, 3))
                    for n in (0, 1):
                        if (unit or start) and ahead(i, t, 1):
                            by_key(*ahead(i, t, 1), n)
                        if unit:
                            values(i, t, n)
                    if (unit or start) and ahead(i, t, 2):
                        top_to_rows(*ahead(i, t, 2))
                    dense(i, t, "b")
                    if (i.base, t) == (FIRST, 11):
                        for n in range(4):
                            ins = nc.tensor.transpose(dense_bank[1][:, n * D:(n + 1) * D], w_nat[:, n * D:(n + 1) * D],
                                                      identity)
                        ins.then_inc(s_wt, 1)
                        pe.wait_ge(s_wt_read, 1)

            pipeline(pe, body)

        @block.vector
        def _(dve):
            steps = [0]

            def step(ins):
                steps[0] += 1
                ins.then_inc(s_step, 1)
                dve.wait_ge(s_step, steps[0])

            def set_up():
                dve.wait_ge(s_const, N_CONST)
                dve.wait_ge(s_late, N_LATE)
                dve.wait_ge(s_setup, N_FILLS)
                nc.vector.tensor_copy(cstb[:], cst[:, CW:CW + CWB]).then_inc(s_cast, 1)
                nc.vector.tensor_copy(spread[:], spread_in[:].rearrange("p a b -> p (a b)")).then_inc(s_cast, 1)
                for n in (0, 1):
                    nc.vector.tensor_copy(top_row[n][T:P], cst[T:P, CW + C_HQ:CW + C_HQ + 2 * T]).then_inc(s_cast, 1)

            def job(i, name):
                dve.wait_ge(s_job, nth(JOBS, i, name))
                return dense_bank[BANK[name]]

            def flat(a):
                return a[:].rearrange("p t d -> p (t d)")

            def norm_stats(i, name, src):
                for t in range(TILES):
                    ins = nc.vector.bn_stats(stat6[:, t, :], src[:, t, :])
                step(ins)
                for t in range(TILES):
                    ins = nc.vector.bn_aggr(mean_var[name][:, t, :], stat6[:, t, :])
                step(ins)
                nc.vector.tensor_scalar(var_eps[name][:], mean_var[name][:, :, 1], EPS, None,
                                        ALU.add).then_inc(s_var, 1)

            def norm_rows(i, name, src, dst):
                dve.wait_ge(s_rstd, nth(NORMS, i, name))
                for t in range(TILES):
                    ins = nc.vector.tensor_scalar(dst[:, t, :], src[:, t, :], mean_var[name][:, t, 0:1],
                                                  rstd[name][:, t:t + 1], ALU.subtract, ALU.mult)
                ins.then_inc(s_norm, 1)

            def low(i, name, src, bias, hi, lo):
                dve.wait_ge(s_hi, nth(HIGHS, i, name))
                nc.vector.scalar_tensor_tensor(out=lo, in0=src, scalar=cols[:, bias:bias + 1], in1=hi, op0=ALU.add,
                                               op1=ALU.subtract).then_inc(s_dve_job, 1)

            def diagonal(a):
                for s in range(HG):
                    ins = nc.vector.tensor_scalar(
                        q_diag[:, a, :, s, :], q_part[:, a, :].rearrange("p (b q) -> p b q", q=T),
                        hh_mask[:, s:s + 1], None, ALU.mult)
                ins.then_inc(s_diag, 1)

            def take_top(i, t):
                dve.wait_ge(s_scores_q, 2 * nth(UNITS, i, t) - 1)
                w = 4 if layer(t) == 0 else 8
                maxima = top[t % 2][:].rearrange("p n a -> p (n a)")
                for n in (0, 1):
                    if n == 1:
                        dve.wait_ge(s_scores_q, 2 * nth(UNITS, i, t))
                    nc.vector.tensor_reduce(maxima[:, w * n:w * n + w],
                                            query_bank[n][:].rearrange("p (a k) -> p a k", a=w), AX_X, ALU.max,
                                            negate=True).then_inc(s_taken, 1)
                dve.wait_ge(s_taken, 2 * nth(UNITS, i, t))
                step(nc.vector.tensor_copy(top_rep[t % 3][:, 0:2 * w], maxima[:, 0:2 * w]))
                nc.vector.tensor_tensor(top_rep[t % 3][:, 2 * w:4 * w], maxima[:, 0:2 * w],
                                        top_rep[t % 3][:, 0:2 * w], ALU.subtract).then_inc(s_top, 1)

            def normalize(i, t):
                dve.wait_ge(s_side, nth(SIDES, i, ("nat", t)))
                if layer(t - 1) == 0:
                    o, tile = odd(NAT[t], i), place(t - 1) // 2
                    nat = side[:].rearrange("p (s e) -> p s e", s=2)
                    for s in (0, 1):
                        ins = nc.vector.reciprocal(rden[:, 8 * s:8 * s + 8], nat[:, s, VW * s + DH:256:32])
                    step(ins)
                    for s in (0, 1):
                        num = nat[:, s].rearrange("p (a w) -> p a w", w=32)[:, :, VW * s:VW * s + DH]
                        ins = nc.vector.tensor_tensor(
                            o_nat[:, 0, :].rearrange("p (a s d) -> p a s d", s=2, d=DH)[:, :, s, :], num,
                            rden[:, 8 * s:8 * s + 8].unsqueeze(2).broadcast_to([P, PAIRS, DH]), ALU.mult)
                    ins.then_inc(s_side_read, 1)
                    dve.wait_ge(s_side_read, nth(SIDES, i, ("nat", t)))
                    nc.vector.tensor_tensor(x1[o][:, tile, :], x_in[o][:, tile, :], o_nat[:, 0, :],
                                            ALU.add).then_inc(s_x1, 1)
                else:
                    nat = side[:].rearrange("p (h s w) -> p h s w", h=H, s=2)
                    both = rden[:].rearrange("p (h s) -> p h s", s=2)
                    step(nc.vector.reciprocal(both, nat[:, :, :, DH]))
                    for s in (0, 1):
                        ins = nc.vector.tensor_tensor(
                            o_nat[:, s, :].rearrange("p (h d) -> p h d", d=DH), nat[:, :, s, 0:DH],
                            both[:, :, s].unsqueeze(2).broadcast_to([P, H, DH]), ALU.mult)
                    ins.then_inc(s_side_read, 1)

            def by_key_rows(a):
                return a.rearrange("p (b k) -> p b k", k=T)

            def dense(i, t, where):
                o, f = odd("in", i), odd("ffn", i)
                if (t, where) == (0, "a") and runs("out", i):
                    dve.wait_ge(s_dve_job, nth(JOBS, after(i, -1), "q1", "dve"))
                    diagonal(1)
                if (t, where) == (0, "b") and runs("in", i):
                    dve.wait_ge(s_x, 16 * (chunk("in", i) + 1))
                    norm_stats(i, "x", x_in[o])
                if (t, where) == (1, "a") and runs("in", i):
                    if i.base > FIRST:
                        dve.wait_ge(s_job, nth(JOBS, after(i, -1), "q1"))
                    norm_rows(i, "x", x_in[o], normed)
                    low(i, "k_ctx", by_key_rows(job(i, "k_ctx")[:]), BKC, k_part[:, 0, :, 1, :], k_part[:, 1, :, 1, :])
                if (t, where) == (2, "a") and runs("in", i):
                    low(i, "k0", by_key_rows(job(i, "k0")[:]), BK0, k_part[:, 0, :, 0, :], k_part[:, 1, :, 0, :])
                if (t, where) == (2, "b") and runs("in", i):
                    low(i, "q0", job(i, "q0")[:], BQ0, q_part[:, 0], q_part[:, 1])
                    if i.base > 0:
                        dve.wait_ge(s_q1st, FILL * (chunk("out", i) + 1))
                    elif i.base > FIRST:
                        dve.wait_ge(s_qst, FILL * chunk("in", i))
                    diagonal(0)
                if (t, where) == (3, "a") and runs("in", i):
                    dve.wait_ge(s_dve_job, nth(JOBS, i, "q0", "dve"))
                    diagonal(1)
                if t in (3, 4) and where == "ab"[t == 3] and runs("in", i):
                    name, b = ("v0a", "v0b")[t - 3], 4 * (t - 3)
                    nc.vector.tensor_tensor(
                        v0[o][:, b:b + 4, :, 0:DH], job(i, name)[:].rearrange("p (b h d) -> p b h d", b=4, d=DH),
                        row_bv0[:].rearrange("p (h d) -> p h d", d=DH).unsqueeze(1).broadcast_to([P, 4, H, DH]),
                        ALU.add).then_inc(s_dve_job, 1)
                if (t, where) == (5, "a") and runs("ffn", i):
                    dve.wait_ge(s_x1, nth(RESIDUALS, i, 5))
                    norm_stats(i, "x1", x1[f])
                if (t, where) == (5, "b") and runs("ffn", i):
                    if i.base > 0:
                        dve.wait_ge(s_job, nth(JOBS, after(i, -1), "q1"))
                    norm_rows(i, "x1", x1[f], normed_f)
                if (t, where) == (6, "a") and runs("ffn", i):
                    if i.base > 0:
                        dve.wait_ge(s_hi, nth(HIGHS, after(i, -1), "k1"))
                    dve.wait_ge(s_pool, nth(POOLED, i, "keep"))
                    nc.vector.scalar_tensor_tensor(
                        out=k1_full[:], in0=job(i, "k1")[:], scalar=cols[:, BK1:BK1 + 1], in1=keep[:], op0=ALU.add,
                        op1=ALU.mult).then_inc(s_dve_job, 1)
                if (t, where) == (6, "b") and runs("ffn", i):
                    dve.wait_ge(s_pool, nth(POOLED, i, "offset"))
                    norm_stats(i, "x1_again", normed_f)
                if (t, where) == (7, "a") and runs("ffn", i):
                    norm_rows(i, "x1_again", normed_f, normed_f)
                if (t, where) == (8, "b") and runs("ffn", i):
                    dve.wait_ge(s_scores_k, 2 * nth(UNITS, i, 8))
                    dve.wait_ge(s_hi, nth(HIGHS, i, "k1"))
                    nc.vector.tensor_tensor(k1_part[:, 1], k1_full[:], k1_part[:, 0], ALU.subtract).then_inc(s_k1_lo, 1)
                if (t, where) == (9, "b") and runs("ffn", i):
                    dve.wait_ge(s_pool, nth(POOLED, i, "x1_b2"))
                    nc.vector.tensor_tensor(flat(x2[f]), job(i, "w2")[:], flat(x1[f]), ALU.add).then_inc(s_dve_job, 1)
                    dve.wait_ge(s_dve_job, nth(JOBS, i, "w2", "dve"))
                    norm_stats(i, "x2", x2[f])
                if (t, where) == (10, "a") and runs("ffn", i):
                    norm_rows(i, "x2", x2[f], normed_f)
                if (t, where) == (11, "a") and runs("out", i):
                    dve.wait_ge(s_pool, nth(POOLED, after(i, -1), "x2_bo"))
                    if i.base > 1 or i.reg is not None:
                        dve.wait_ge(s_stored, 16 * (chunk("out", i) + 1))
                    nc.vector.tensor_tensor(flat(result), job(i, "out")[:], flat(x2[odd("out", i)]),
                                            ALU.add).then_inc(s_dve_job, 1)
                if (t, where) == (11, "b") and runs("ffn", i):
                    low(i, "q1", job(i, "q1")[:], BQ1, q_part[:, 0], q_part[:, 1])
                    dve.wait_ge(s_qst, FILL * (chunk("in", i) + 1 if runs("in", i) else CHUNKS))
                    diagonal(0)

            def body(i):
                steps[0] = 0
                for t in range(SLOTS):
                    unit = runs(unit_stage(t), i) or (i.base, t) in STARTS
                    if (i.base, t) == (FIRST, 8):
                        set_up()
                    if (i.base, t) in STARTS:
                        take_top(i, t + 1)
                        take_top(i, t + 2)
                    if t in NAT and runs(NAT[t], i):
                        normalize(i, t)
                    dense(i, t, "a")
                    if unit and ahead(i, t, 3):
                        take_top(*ahead(i, t, 3))
                    dense(i, t, "b")
                dve.sem_clear(s_step)

            pipeline(dve, body)


_INS = ["x", "ctx_1024", "mask_BxS2_ik0", "L0_xattn_w_qkv", "L0_xattn_b_qkv", "L0_xattn_w_ckv", "L0_xattn_b_ckv",
        "L0_xattn_g1", "L0_xattn_be1", "L0_xattn_g2", "L0_xattn_be2", "L0_xattn_gf", "L0_xattn_bf", "L0_xattn_w1",
        "L0_xattn_b1", "L0_xattn_w2", "L0_xattn_b2", "L1_xattn_ln_w", "L1_xattn_ln_b", "L1_xattn_wq", "L1_xattn_bq",
        "L1_xattn_wk", "L1_xattn_bk", "L1_xattn_wv", "L1_xattn_bv", "L1_xattn_wo", "L1_xattn_bo"]


def kernel(**inputs):
    import numpy as _np
    import concourse.bacc as _bacc
    from concourse import mybir as _mybir
    from concourse.bass_utils import run_bass_kernel_spmd as _run

    nc = _bacc.Bacc("TRN2", target_bir_lowering=False, num_devices=1)
    arrays, io = {}, {}
    for name in _INS + ["constants"]:
        a = _np.ascontiguousarray(constants() if name == "constants" else inputs[name])
        arrays[f"in_{name}"] = a
        io[name] = nc.dram_tensor(f"in_{name}", a.shape, _mybir.dt.from_np(a.dtype), kind="ExternalInput").ap()
    out = nc.dram_tensor("out_0", (B, T, D), F32, kind="ExternalOutput").ap()
    xattn_program(nc, io, io.pop("constants"), out)
    r = _run(nc, [arrays], core_ids=[0])
    return r.results[0]["out_0"]
```

```python
from collections import namedtuple
from contextlib import ExitStack

import concourse.bass as bass
from concourse import mybir

ALU = mybir.AluOpType
ACT = mybir.ActivationFunctionType
AX_X = mybir.AxisListType.X
F32 = mybir.dt.float32
F16 = mybir.dt.float16
BF16 = mybir.dt.bfloat16
I32 = mybir.dt.int32

P = 128
B, T, D = 64, 64, 128
H, DH, F = 16, 8, 512
CB = 8
CHUNKS = B // CB
TOK = CB * T
TILES = TOK // P
FC = F // P
G = 4
HG = H // G
PARTS = 2
TERMS = 3
ROWS = TERMS * HG * DH
Q_PART = (0, 0, 1)
K_PART = (0, 1, 0)
PAIRS = H // 2
VW = 16
TOPS = 32
EPS = 1e-5
SCALE = float(DH) ** -0.5
CAUSAL = -1e30
N_VEC = 12 + FC
KEYMASK = 32768.0
POOL_GROUPS = 1
SP_FILLS, POOL_FILLS = TERMS * (G - POOL_GROUPS), TERMS * POOL_GROUPS

Body = namedtuple("Body", "reg base")
FIRST, LAST = -1, CHUNKS
SLOTS = 12
STARTS = ((FIRST, 8), (0, 8), (LAST, 4))
LAG = {"in": -1, "ffn": 0, "out": 1}


def after(i, n=1):
    return Body(i.reg, i.base + n)


def chunk(stage, i):
    return i.base - LAG[stage] + (0 if i.reg is None else i.reg)


def odd(stage, i):
    return (i.base - LAG[stage]) % 2


def runs(stage, i):
    return i.reg is not None or 0 <= i.base - LAG[stage] < CHUNKS


def unit_stage(t):
    return "ffn" if t < 5 else "out" if t < 9 else "in"


def layer(t):
    return 1 if 5 <= t < 9 else 0


def place(t):
    return t + 3 if t < 5 else t - 5 if t < 9 else t - 9


def ahead(i, t, n):
    for _ in range(n):
        i, t = (after(i), 0) if t == SLOTS - 1 else (i, t + 1)
        if not runs(unit_stage(t), i):
            return None
    return i, t


JOB_LIST = [
    ("ctx_t", 0, "b", "in", "act"), ("k_ctx", 1, "b", "in", "dve"),
    ("x_t", 2, "a", "in", "act"), ("k0", 2, "b", "in", "dve"),
    ("q0", 3, "a", "in", "dve"),
    ("v0a", 3, "b", "in", "dve"), ("v0b", 4, "a", "in", "dve"),
    ("k1", 6, "a", "ffn", "dve"), ("f_t", 7, "b", "ffn", "act"),
    ("w1_0", 8, "b", "ffn", "act"), ("w1_1", 8, "b", "ffn", "act"),
    ("w1_2", 8, "b", "ffn", "act"), ("w1_3", 8, "b", "ffn", "act"),
    ("v1", 9, "a", "ffn", "act"), ("w2", 9, "b", "ffn", "dve"),
    ("out", 11, "a", "out", "dve"), ("x2_t", 11, "a", "ffn", "act"),
    ("q1", 11, "b", "ffn", "dve")]
JOBS = [(name, stage) for name, _, _, stage, _ in JOB_LIST]
BANK = {name: n % 2 for n, (name, _) in enumerate(JOBS)}
READER = {name: who for name, _, _, _, who in JOB_LIST}
UNITS = [(t, unit_stage(t)) for t in range(SLOTS)]
NORMS = [("x", "in"), ("x1", "ffn"), ("x1_again", "ffn"), ("x2", "ffn")]
HIGHS = [("k_ctx", "in"), ("k0", "in"), ("q0", "in"), ("k1", "ffn"), ("q1", "ffn")]
DIAGS = [("q0", "in"), ("q1", "ffn")]
NAT = {1: "ffn", 3: "ffn", 5: "ffn", 7: "out", 9: "out", 11: "in"}
BACK = (8, 10)
RESIDUALS = [(t, NAT[t]) for t in (1, 3, 5, 11)]
POOLED = [("keep", "ffn"), ("mask_row", "ffn"), ("gain", "ffn"), ("offset", "ffn"), ("x1_b2", "ffn"),
          ("x2_bo", "ffn")]
SIDES = []
for _t in range(SLOTS):
    if _t in NAT:
        SIDES.append((("nat", _t), NAT[_t]))
    if _t in BACK:
        SIDES.append((("back", _t), "out"))


def happens(name, stage, b):
    return runs(stage, Body(None, b))


def nth(events, i, name, who=None):
    names = [e[0] for e in events]

    def upto(b):
        whole = sum(happens(n, s, a) for a in range(FIRST, b) for n, s in events if who in (None, READER.get(n)))
        part = [e for e in events[:names.index(name) + 1] if who in (None, READER.get(e[0]))]
        return whole + sum(happens(n, s, b) for n, s in part if b >= FIRST)

    n = upto(i.base)
    if i.reg is None:
        return n
    period = len([e for e in events if who in (None, READER.get(e[0]))])
    assert n > 0 and upto(i.base + 1) - n == period
    return i.reg * period + n


def some(count):
    return not isinstance(count, int) or count > 0


def jobs_before(i, name):
    names = [n for n, _ in JOBS]
    n = names.index(name) - 2
    if n < 0:
        i, n = after(i, -1), n + len(names)
    for who in ("act", "dve"):
        older = [m for m in names[:n + 1] if READER[m] == who]
        if READER[names[n]] == who or (i.reg is None and older):
            yield i, older[-1], who


C_ID, C_HH = 0, P
CW = P + HG
C_IDB, C_EQ, C_HK, C_HQ = 0, P, 2 * P, 2 * P + T
CWB = C_HQ + 2 * T
C_S0 = 0
C_S1 = PAIRS * P
CWS = 2 * PAIRS * P


def constants():
    import numpy as np

    p = np.arange(P)[:, None]
    c = np.arange(P)[None, :]
    k = np.arange(T)[None, :]
    out = np.zeros((P, CW + CWB + CWS), np.float32)
    out[:, C_ID:C_ID + P] = p == c
    out[:, C_HH:C_HH + HG] = p % (HG * DH) // DH == np.arange(HG)
    b = out[:, CW:CW + CWB]
    b[:, C_IDB:C_IDB + P] = p == c
    b[:, C_EQ:C_EQ + P] = (p == c % T) & (p < T)
    b[:, C_HK:C_HK + T] = np.where((k > p) & (p < T), CAUSAL, 0.0)
    b[:, C_HQ:C_HQ + 2 * T] = np.where((p - T > c % T), CAUSAL, 0.0)
    s = out[:, CW + CWB:]
    for a in range(PAIRS):
        s[:, C_S0 + P * a:C_S0 + P * a + P] = ((p < 16) & (p % PAIRS == a)) | (p - T == c)
        s[:, C_S1 + P * a:C_S1 + P * a + P] = (p < TOPS) & (p % PAIRS == a) & (p // PAIRS % 2 == c // T)
    return out


def xattn_program(nc, io, consts, out):
    ctx = ExitStack()
    with ctx:
        def sb(name, shape, dt=F32):
            return ctx.enter_context(nc.sbuf_tensor(name, shape, dt))

        def two(name, shape, dt=F32):
            return [sb(f"{name}{n}", shape, dt) for n in (0, 1)]

        def sem(name):
            return ctx.enter_context(nc.semaphore(name))

        w_qkv = sb("w_qkv", [P, 3 * D])
        w_ckv = sb("w_ckv", [P, 2 * D])
        w1 = sb("w1", [P, F])
        w2 = sb("w2", [P, FC, D])
        w_t = sb("w_t", [P, 4, D])
        vectors = sb("vectors", [N_VEC, P])
        cols = sb("cols", [P, N_VEC])
        (G1, BE1, GF, BF, LW, LB, BQ0, BK0, BKC, BQ1, BK1, BV1) = range(12)
        B1 = 12
        row_g2 = sb("row_g2", [P, D])
        row_be2 = sb("row_be2", [P, D])
        row_b2 = sb("row_b2", [P, D])
        row_bv0 = sb("row_bv0", [P, D])
        row_bo = sb("row_bo", [P, D])
        half = sb("half", [P, TILES])
        spare = sb("spare", [P, 4])
        cst = sb("cst", [P, CW + CWB])
        cstb = sb("cstb", [P, CWB], BF16)
        spread = sb("spread", [P, CWS], BF16)
        identity = cst[:, C_ID:C_ID + P]
        hh_mask = cst[:, C_HH:C_HH + HG]
        identity_b = cstb[:, C_IDB:C_IDB + P]
        eye_query = cstb[:, C_EQ:C_EQ + P]
        hide_key = cstb[:, C_HK:C_HK + T]

        x_in = two("x_in", [P, TILES, D])
        ctx_in = sb("ctx_in", [P, TILES, D])
        normed = sb("normed", [P, TILES, D])
        normed_t = sb("normed_t", [P, TOK])
        normed_f = sb("normed_f", [P, TILES, D])
        normed_ft = sb("normed_ft", [P, TOK])
        ctx_t = two("ctx_t", [P, TOK])
        q_part = sb("q_part", [P, PARTS, TOK], F16)
        q_diag = sb("q_diag", [P, PARTS, CB, HG, T], F16)
        k_part = sb("k_part", [P, PARTS, CB, 2, T], F16)
        k1_part = sb("k1_part", [P, PARTS, TOK], F16)
        q_stack = two("q_stack", [P, G, CB, HG * T], F16)
        k_stack = two("k_stack", [P, G, CB, 2 * T], F16)
        q1_stack = sb("q1_stack", [P, G, CB, HG * T], F16)
        k1_stack = sb("k1_stack", [P, G, TOK], F16)
        v0 = two("v0", [P, CB, H, VW])
        v1 = sb("v1", [P, TILES, H, 2, VW])
        probs = two("probs", [P, H, T])
        top = two("top", [P, 2, PAIRS])
        top_rep = [sb(f"top_rep{n}", [P, TOPS], BF16) for n in range(3)]
        top_row = two("top_row", [P, P], BF16)
        stat6 = sb("stat6", [P, TILES, 6])
        mean_var = {n: sb(f"mean_var_{n}", [P, TILES, 2]) for n, _ in NORMS}
        var_eps = {n: sb(f"var_eps_{n}", [P, TILES]) for n, _ in NORMS}
        rstd = {n: sb(f"rstd_{n}", [P, TILES]) for n, _ in NORMS}
        o_t = sb("o_t", [P, 4, 2, T])
        rden = sb("rden", [P, 32])
        o_nat = sb("o_nat", [P, 2, D])
        x1 = two("x1", [P, TILES, D])
        x2 = two("x2", [P, TILES, D])
        hidden = sb("hidden", [P, FC, TOK])
        k1_full = sb("k1_full", [P, TOK])
        mix_t = sb("mix_t", [P, TOK])
        mask_in = sb("mask_in", [P, TOK], I32)
        keep = sb("keep", [P, TOK])
        mask_row = two("mask_row", [P, TOK], F16)
        result = sb("result", [P, TILES, D])
        w_nat = k1_full
        spread_in = hidden

        bank = [ctx.enter_context(nc.psum_tensor(f"bank{n}", [P, 512], F32)) for n in range(8)]
        query_bank, key_bank, dense_bank, side, mixed = bank[0:2], bank[2:4], bank[4:6], bank[6], bank[7]
        turned = mixed[0:TOPS, 256:256 + P // 2].bitcast(BF16)

        s_const = sem("s_const")
        s_late = sem("s_late")
        s_cols = sem("s_cols")
        s_cols_read = sem("s_cols_read")
        s_wt = sem("s_wt")
        s_wt_read = sem("s_wt_read")
        s_setup = sem("s_setup")
        s_half = sem("s_half")
        s_stacks = sem("s_stacks")
        s_cast = sem("s_cast")
        s_x = sem("s_x")
        s_ctx = sem("s_ctx")
        s_mask = sem("s_mask")
        s_taken = sem("s_taken")
        s_var = sem("s_var")
        s_rstd = sem("s_rstd")
        s_norm = sem("s_norm")
        s_job = sem("s_job")
        s_act_job = sem("s_act_job")
        s_dve_job = sem("s_dve_job")
        s_hi = sem("s_hi")
        s_diag_hi = sem("s_diag_hi")
        s_diag = sem("s_diag")
        s_k1_lo = sem("s_k1_lo")
        s_fill = {n: sem(f"s_fill_{n}") for n in ("k", "q", "k1", "q1")}
        s_pool_fill = {n: sem(f"s_pool_fill_{n}") for n in ("k", "q", "k1", "q1")}
        s_pool = sem("s_pool")
        s_scores_q = sem("s_scores_q")
        s_top = sem("s_top")
        s_turned = sem("s_turned")
        s_row = sem("s_row")
        s_scores_k = sem("s_scores_k")
        s_probs = sem("s_probs")
        s_mixed = sem("s_mixed")
        s_o_t = sem("s_o_t")
        s_side = sem("s_side")
        s_side_read = sem("s_side_read")
        s_x1 = sem("s_x1")
        s_stored = sem("s_stored")
        s_step = sem("s_step")

        tokens = lambda a: a.rearrange("(c t b) q d -> c (b q) t d", c=CHUNKS, b=2)
        x_d, ctx_d, out_d = tokens(io["x"]), tokens(io["ctx_1024"]), tokens(out)
        mask_d = io["mask_BxS2_ik0"].rearrange("(c b) k -> c (b k)", c=CHUNKS)
        block = ctx.enter_context(nc.Block())

        def across(v):
            return v.partition_broadcast(P)

        col_of = [("L0_xattn_g1", 0), ("L0_xattn_be1", 0), ("L0_xattn_gf", 0), ("L0_xattn_bf", 0),
                  ("L1_xattn_ln_w", 0), ("L1_xattn_ln_b", 0), ("L0_xattn_b_qkv", 0),
                  ("L0_xattn_b_qkv", D), ("L0_xattn_b_ckv", 0), ("L1_xattn_bq", 0),
                  ("L1_xattn_bk", 0), ("L1_xattn_bv", 0)]
        first_loads = [(cst[:], consts[:, 0:CW + CWB])]
        first_loads += [(vectors[n:n + 1, :], io[v][o:o + D].rearrange("(a p) -> a p", a=1))
                        for n, (v, o) in enumerate(col_of)]
        first_loads += [(vectors[B1:B1 + FC, :], io["L0_xattn_b1"].rearrange("(c p) -> c p", p=P)),
                        (w_ckv[:], io["L0_xattn_w_ckv"]), (w_qkv[:], io["L0_xattn_w_qkv"]),
                        (row_bv0[0:T], io["L0_xattn_b_qkv"][2 * D:3 * D].partition_broadcast(T)),
                        (row_bv0[T:P], io["L0_xattn_b_ckv"][D:2 * D].partition_broadcast(T))]
        late_loads = [(spread_in[:].rearrange("p a b -> p (a b)"), consts[:, CW + CWB:CW + CWB + CWS])]
        late_loads += [(w_nat[:, n * D:(n + 1) * D], io[f"L1_xattn_{w}"])
                       for n, w in enumerate(("wq", "wk", "wv", "wo"))]
        late_loads += [(w1[:], io["L0_xattn_w1"]), (w2[:], io["L0_xattn_w2"].rearrange("(c p) n -> p c n", p=P)),
                       (row_g2[:], across(io["L0_xattn_g2"])), (row_be2[:], across(io["L0_xattn_be2"])),
                       (row_b2[:], across(io["L0_xattn_b2"])), (row_bo[:], across(io["L1_xattn_bo"]))]
        N_CONST, N_LATE = 16 * len(first_loads), 16 * len(late_loads)

        N_STACKS = 6
        memsets = [(v0[0][:], 0.0), (v0[1][:], 0.0)]
        memsets += [(top_row[n][:], 0.0) for n in (0, 1)] + [(top_rep[n][:], 0.0) for n in range(3)]
        memsets += [(v0[n][:, :, :, DH:DH + 1], 1.0) for n in (0, 1)]

        def fill(queue, name, stack, terms=range(TERMS)):
            ours = range(G - POOL_GROUPS) if queue is nc.sync else range(G - POOL_GROUPS, G)
            filled = (s_fill if queue is nc.sync else s_pool_fill)[name]
            part, order = {"k": (k_part[:].rearrange("p a b s k -> p a b (s k)"), K_PART), "k1": (k1_part, K_PART),
                           "q": (q_diag[:].rearrange("p a b h q -> p a b (h q)"), Q_PART),
                           "q1": (q_diag[:].rearrange("p a b h q -> p a b (h q)"), Q_PART)}[name]
            for t in terms:
                for g in ours:
                    rows = slice(HG * DH * g, HG * DH * (g + 1))
                    queue.dma_start(stack[HG * DH * t:HG * DH * (t + 1), g], part[rows, order[t]]).then_inc(filled, 16)

        def pipeline(engine, body):
            body(Body(None, -1))
            body(Body(None, 0))
            with engine.Fori(0, CHUNKS - 3, 2) as r:
                body(Body(r, 1))
                body(Body(r, 2))
            body(Body(None, CHUNKS - 1))
            body(Body(None, CHUNKS))

        @block.sync
        def _(sp):
            def body(i):
                if runs("in", i):
                    c = chunk("in", i)
                    n_before = nth(RESIDUALS, after(i, -1), 5)
                    if some(n_before):
                        sp.wait_ge(s_x1, n_before)
                    sp.dma_start(x_in[odd("in", i)][:], x_d[c]).then_inc(s_x, 16)
                    if i.base != FIRST:
                        sp.wait_ge(s_act_job, nth(JOBS, after(i, -1), "ctx_t", "act"))
                    sp.dma_start(ctx_in[:], ctx_d[c]).then_inc(s_ctx, 16)
                if i.base == FIRST:
                    for dst, src in first_loads[1::2]:
                        sp.dma_start(dst, src).then_inc(s_const, 16)
                if runs("ffn", i):
                    n_before = nth(POOLED, after(i, -1), "mask_row")
                    if some(n_before):
                        sp.wait_ge(s_pool, n_before)
                    sp.dma_start(mask_in[:], mask_d[chunk("ffn", i)].partition_broadcast(P)).then_inc(s_mask, 16)
                if runs("out", i):
                    sp.wait_ge(s_diag_hi, nth(DIAGS, after(i, -1), "q1"))
                    fill(nc.sync, "q1", q1_stack, (0, 1))
                    sp.wait_ge(s_diag, nth(DIAGS, after(i, -1), "q1"))
                    fill(nc.sync, "q1", q1_stack, (2,))
                if runs("in", i):
                    sp.wait_ge(s_dve_job, nth(JOBS, i, "k0", "dve"))
                    fill(nc.sync, "k", k_stack[odd("in", i)])
                    sp.wait_ge(s_diag_hi, nth(DIAGS, i, "q0"))
                    fill(nc.sync, "q", q_stack[odd("in", i)], (0, 1))
                    sp.wait_ge(s_diag, nth(DIAGS, i, "q0"))
                    fill(nc.sync, "q", q_stack[odd("in", i)], (2,))
                if runs("ffn", i):
                    sp.wait_ge(s_k1_lo, chunk("ffn", i) + 1)
                    fill(nc.sync, "k1", k1_stack)
                    if i.base == 0:
                        sp.wait_ge(s_stacks, N_STACKS)
                    row = mask_row[odd("ffn", i)][ROWS:ROWS + 1]
                    sp.dma_start(k1_stack[ROWS:ROWS + 1],
                                 row.unsqueeze(1).broadcast_to([1, G, TOK])).then_inc(s_fill["k1"], 16)
                if runs("out", i):
                    sp.wait_ge(s_dve_job, nth(JOBS, i, "out", "dve"))
                    sp.dma_start(out_d[chunk("out", i)], result[:]).then_inc(s_stored, 16)

            pipeline(sp, body)
            sp.wait_ge(s_stored, 16 * (CHUNKS + 1))

        @block.gpsimd
        def _(pool):
            fills = [(v1[:], 0.0), (v1[0:T, :, :, 0, DH:DH + 1], 1.0), (v1[T:P, :, :, 1, DH:DH + 1], 1.0),
                     (k1_stack[ROWS:P], 0.0), (q1_stack[ROWS:P], 0.0), (q1_stack[ROWS:ROWS + 1], KEYMASK)]

            def set_up():
                for n, (dst, value) in enumerate(fills):
                    nc.gpsimd.memset(dst, value).then_inc(s_stacks, 1)
                    pool.wait_ge(s_stacks, n + 1)

            def carry_wait(at):
                nc.gpsimd.tensor_tensor(spare[:, at:at + 1], half[:, 0:1], half[:, 1:2], ALU.mult)

            def root(i, name):
                pool.wait_ge(s_var, nth(NORMS, i, name))
                nc.gpsimd.tensor_tensor(rstd[name][:], var_eps[name][:], half[:], ALU.pow).then_inc(s_rstd, 1)

            def rows(v):
                return v[:].unsqueeze(1).broadcast_to([P, TILES, D])

            def body(i):
                if i.base == FIRST:
                    for dst, src in late_loads:
                        nc.gpsimd.dma_start(dst, src).then_inc(s_late, 16)
                    nc.gpsimd.memset(half[:], -0.5).then_inc(s_half, 1)
                    pool.wait_ge(s_half, 1)
                    nc.gpsimd.memset(spare[:], 0.0).then_inc(s_stored, 16)
                    pool.wait_ge(s_stored, 16)
                if runs("out", i):
                    pool.wait_ge(s_diag, nth(DIAGS, after(i, -1), "q1"))
                    carry_wait(0)
                    fill(nc.gpsimd, "q1", q1_stack)
                if runs("ffn", i):
                    pool.wait_ge(s_mask, 16 * (chunk("ffn", i) + 1))
                    pool.wait_ge(s_dve_job, nth(JOBS, after(i, -1), "q1", "dve"))
                if runs("in", i):
                    root(i, "x")
                if i.base == 0:
                    pool.wait_ge(s_late, N_LATE)
                if runs("ffn", i):
                    o = odd("ffn", i)
                    nc.gpsimd.tensor_scalar(keep[:], mask_in[:], 0, 0, ALU.is_equal, ALU.is_equal).then_inc(s_pool, 1)
                    nc.gpsimd.tensor_scalar(mask_row[o][:], mask_in[:], 0, -KEYMASK, ALU.is_equal,
                                            ALU.mult).then_inc(s_pool, 1)
                if runs("in", i):
                    pool.wait_ge(s_dve_job, nth(JOBS, i, "k0", "dve"))
                    carry_wait(1)
                    fill(nc.gpsimd, "k", k_stack[odd("in", i)])
                    pool.wait_ge(s_diag, nth(DIAGS, i, "q0"))
                    carry_wait(2)
                    fill(nc.gpsimd, "q", q_stack[odd("in", i)])
                if i.base == FIRST:
                    set_up()
                if runs("ffn", i):
                    root(i, "x1")
                    pool.wait_ge(s_norm, nth(NORMS, i, "x1"))
                    nc.gpsimd.tensor_tensor(normed_f[:], normed_f[:], rows(row_g2), ALU.mult).then_inc(s_pool, 1)
                    pool.wait_ge(s_pool, nth(POOLED, i, "gain"))
                    nc.gpsimd.tensor_tensor(normed_f[:], normed_f[:], rows(row_be2), ALU.add).then_inc(s_pool, 1)
                    root(i, "x1_again")
                    nc.gpsimd.tensor_tensor(x1[o][:], x1[o][:], rows(row_b2), ALU.add).then_inc(s_pool, 1)
                    pool.wait_ge(s_k1_lo, chunk("ffn", i) + 1)
                    carry_wait(3)
                    fill(nc.gpsimd, "k1", k1_stack)
                    root(i, "x2")
                    pool.wait_ge(s_norm, nth(NORMS, i, "x2"))
                    nc.gpsimd.tensor_tensor(x2[o][:], x2[o][:], rows(row_bo), ALU.add).then_inc(s_pool, 1)

            pipeline(pool, body)

        @block.scalar
        def _(act):
            def job(i, name):
                act.wait_ge(s_job, nth(JOBS, i, name))
                return dense_bank[BANK[name]]

            def exp(i, t):
                for n in (0, 1):
                    act.wait_ge(s_scores_k, 2 * nth(UNITS, i, t) - 1 + n)
                    nc.scalar.activation(
                        probs[t % 2][:, 8 * n:8 * n + 8].rearrange("p h q -> p (h q)"), key_bank[n][:],
                        ACT.Exp, scale=SCALE).then_inc(s_probs, 1)

            def copy_rows(i, t):
                act.wait_ge(s_turned, nth(UNITS, i, t))
                nc.scalar.copy(top_row[t % 2][0:TOPS], turned).then_inc(s_row, 1)

            def copy_mixed(i, t):
                act.wait_ge(s_mixed, nth(UNITS, i, t))
                if ahead(i, t, 2):
                    act.wait_ge(s_turned, nth(UNITS, *ahead(i, t, 2)))
                if t % 2:
                    act.wait_ge(s_side, nth(SIDES, i, ("nat", t)))
                half_of = (t + 1) % 2
                if layer(t) == 0:
                    dst = o_t[:, :, half_of, :].rearrange("p (s a) q -> p a s q", s=2)
                    src = mixed[:, 0:256].rearrange("p (a s q) -> p a s q", a=2, s=2)
                else:
                    dst = o_t[:, :, half_of, :]
                    src = mixed[:, 0:256].rearrange("p (g q) -> p g q", g=G)
                nc.scalar.copy(dst, src).then_inc(s_o_t, 1)

            def mix(i, t):
                act.wait_ge(s_side, nth(SIDES, i, ("back", t)))
                if i.base > 0:
                    act.wait_ge(s_job, nth(JOBS, after(i, -1), "q1"))
                at = 2 * P * BACK.index(t)
                nc.scalar.activation(
                    mix_t[:, at:at + 2 * P].rearrange("p (t s q) -> p s t q", t=2, s=2),
                    side[:, 0:2 * P].rearrange("p (s t q) -> p s t q", s=2, t=2), ACT.Identity,
                    bias=cols[:, BV1:BV1 + 1]).then_inc(s_side_read, 1)

            def high(i, name, dst, src, bias):
                nc.scalar.activation(dst, src, ACT.Identity, bias=cols[:, bias:bias + 1]).then_inc(s_hi, 1)

            def keys(name, i):
                return job(i, name)[:].rearrange("p (b k) -> p b k", k=T)

            def scaled(i, name, dst, gain, offset):
                nc.scalar.activation(dst[:], job(i, name)[:], ACT.Identity, scale=cols[:, gain:gain + 1],
                                     bias=cols[:, offset:offset + 1]).then_inc(s_act_job, 1)

            def dense(i, t, where):
                if (t, where) == (0, "b") and runs("in", i):
                    nc.scalar.copy(ctx_t[odd("in", i)][:], job(i, "ctx_t")[:]).then_inc(s_act_job, 1)
                if (t, where) == (1, "b") and runs("in", i):
                    if i.base > FIRST:
                        act.wait_ge(s_fill["k"], 16 * SP_FILLS * chunk("in", i))
                        act.wait_ge(s_pool_fill["k"], 16 * POOL_FILLS * chunk("in", i))
                    high(i, "k_ctx", k_part[:, 0, :, 1, :], keys("k_ctx", i), BKC)
                if (t, where) == (2, "a") and runs("in", i):
                    scaled(i, "x_t", normed_t, G1, BE1)
                if (t, where) == (2, "b") and runs("in", i):
                    high(i, "k0", k_part[:, 0, :, 0, :], keys("k0", i), BK0)
                if (t, where) == (3, "a") and runs("in", i):
                    n_before = nth(DIAGS, after(i, -1), "q1")
                    if some(n_before):
                        act.wait_ge(s_diag, n_before)
                    high(i, "q0", q_part[:, 0], job(i, "q0")[:], BQ0)
                if (t, where) == (6, "a") and runs("ffn", i):
                    act.wait_ge(s_dve_job, nth(JOBS, i, "k1", "dve"))
                    if i.base > 0:
                        act.wait_ge(s_fill["k1"], 16 * (SP_FILLS + 1) * chunk("ffn", i))
                        act.wait_ge(s_pool_fill["k1"], 16 * POOL_FILLS * chunk("ffn", i))
                    nc.scalar.copy(k1_part[:, 0], k1_full[:]).then_inc(s_hi, 1)
                if (t, where) == (7, "b") and runs("ffn", i):
                    scaled(i, "f_t", normed_ft, GF, BF)
                if (t, where) == (8, "b") and runs("ffn", i):
                    if i.base > 0:
                        act.wait_ge(s_job, nth(JOBS, after(i, -1), "q1"))
                    for f in range(FC):
                        nc.scalar.activation(hidden[:, f, :], job(i, f"w1_{f}")[:], ACT.Gelu,
                                             bias=cols[:, B1 + f:B1 + f + 1]).then_inc(s_act_job, 1)
                if (t, where) == (9, "a") and runs("ffn", i):
                    if i.base == 0:
                        act.wait_ge(s_stacks, N_STACKS)
                    src = job(i, "v1")[:].rearrange("p (t h d) -> p t h d", t=TILES, d=DH)
                    for s in (0, 1):
                        r = slice(T * s, T * s + T)
                        ins = nc.scalar.copy(v1[r, :, :, s, 0:DH], src[r])
                    ins.then_inc(s_act_job, 1)
                if (t, where) == (11, "a") and runs("ffn", i):
                    scaled(i, "x2_t", normed_ft, LW, LB)
                if (t, where) == (11, "b") and runs("ffn", i):
                    act.wait_ge(s_diag, nth(DIAGS, i, "q0"))
                    high(i, "q1", q_part[:, 0], job(i, "q1")[:], BQ1)

            def body(i):
                for t in range(SLOTS):
                    unit = runs(unit_stage(t), i)
                    start = (i.base, t) in STARTS
                    if start:
                        copy_rows(i, t + 1)
                    if t in BACK and runs("out", i):
                        mix(i, t)
                    dense(i, t, "a")
                    if (unit or start) and ahead(i, t, 1):
                        exp(*ahead(i, t, 1))
                    if unit:
                        copy_mixed(i, t)
                    if (unit or start) and ahead(i, t, 2):
                        copy_rows(*ahead(i, t, 2))
                    dense(i, t, "b")
                    if (i.base, t) == (FIRST, 11):
                        act.wait_ge(s_wt, 1)
                        nc.scalar.copy(w_t[:].rearrange("p w n -> p (w n)"), dense_bank[1][:]).then_inc(s_wt_read, 1)

            for dst, src in first_loads[0::2]:
                nc.scalar.dma_start(dst, src).then_inc(s_const, 16)
            act.wait_ge(s_cols, 1)
            nc.scalar.copy(cols[:], query_bank[1][:, 0:N_VEC]).then_inc(s_cols_read, 1)
            act.wait_ge(s_cols_read, 1)
            pipeline(act, body)

        @block.tensor
        def _(pe):
            pe.wait_ge(s_const, N_CONST)
            nc.tensor.transpose(query_bank[1][:, 0:N_VEC], vectors[:], cst[0:N_VEC, C_ID:C_ID + N_VEC]).then_inc(
                s_cols, 1)
            pe.wait_ge(s_cols_read, 1)

            def open_job(i, name):
                for j, other, who in jobs_before(i, name):
                    n_before = nth(JOBS, j, other, who)
                    if some(n_before):
                        pe.wait_ge(s_act_job if who == "act" else s_dve_job, n_before)
                return dense_bank[BANK[name]]

            def transposes(i, name, src):
                b = open_job(i, name)
                for n in range(TILES):
                    ins = nc.tensor.transpose(b[:, n * P:(n + 1) * P], src[:, n, :], identity)
                ins.then_inc(s_job, 1)

            def product(i, name, w, src):
                b = open_job(i, name)
                nc.tensor.matmul(b[:], w, src[:], start=True, stop=True).then_inc(s_job, 1)

            def by_tokens(i, name, src_t, w):
                b = open_job(i, name)
                for n in range(TILES):
                    ins = nc.tensor.matmul(b[:, n * D:(n + 1) * D], src_t[:, n * P:(n + 1) * P], w, start=True,
                                           stop=True)
                ins.then_inc(s_job, 1)

            def dense(i, t, where):
                o = odd("in", i)
                if (t, where) == (0, "b") and runs("in", i):
                    pe.wait_ge(s_ctx, 16 * (chunk("in", i) + 1))
                    transposes(i, "ctx_t", ctx_in)
                if (t, where) == (1, "b") and runs("in", i):
                    pe.wait_ge(s_act_job, nth(JOBS, i, "ctx_t", "act"))
                    product(i, "k_ctx", w_ckv[:, 0:D], ctx_t[o])
                if (t, where) == (2, "a") and runs("in", i):
                    pe.wait_ge(s_norm, nth(NORMS, i, "x"))
                    transposes(i, "x_t", normed)
                if (t, where) == (2, "b") and runs("in", i):
                    pe.wait_ge(s_act_job, nth(JOBS, i, "x_t", "act"))
                    product(i, "k0", w_qkv[:, D:2 * D], normed_t)
                if (t, where) == (3, "a") and runs("in", i):
                    product(i, "q0", w_qkv[:, 0:D], normed_t)
                if (t, where) in ((3, "b"), (4, "a")) and runs("in", i):
                    name = ("v0a", "v0b")[t - 3]
                    b = open_job(i, name)
                    for n in range(4):
                        at = slice((4 * (t - 3) + n) * T, (4 * (t - 3) + n + 1) * T)
                        nc.tensor.matmul(b[0:T, n * D:(n + 1) * D], normed_t[:, at], w_qkv[:, 2 * D:3 * D],
                                         start=True, stop=True)
                        ins = nc.tensor.matmul(b[T:P, n * D:(n + 1) * D], ctx_t[o][:, at], w_ckv[:, D:2 * D],
                                               start=True, stop=True)
                    ins.then_inc(s_job, 1)
                if (t, where) == (6, "a") and runs("ffn", i):
                    product(i, "k1", w_t[:, 1, :], ctx_t[odd("ffn", i)])
                if (t, where) == (7, "b") and runs("ffn", i):
                    pe.wait_ge(s_norm, nth(NORMS, i, "x1_again"))
                    transposes(i, "f_t", normed_f)
                if (t, where) == (8, "b") and runs("ffn", i):
                    pe.wait_ge(s_act_job, nth(JOBS, i, "f_t", "act"))
                    for f in range(FC):
                        product(i, f"w1_{f}", w1[:, f * P:(f + 1) * P], normed_ft)
                if (t, where) == (9, "a") and runs("ffn", i):
                    by_tokens(i, "v1", ctx_t[odd("ffn", i)], w_t[:, 2, :])
                if (t, where) == (9, "b") and runs("ffn", i):
                    b = open_job(i, "w2")
                    for n in range(TILES):
                        for f in range(FC):
                            ins = nc.tensor.matmul(b[:, n * D:(n + 1) * D], hidden[:, f, n * P:(n + 1) * P],
                                                   w2[:, f, :], start=(f == 0), stop=(f == FC - 1))
                    ins.then_inc(s_job, 1)
                if (t, where) == (11, "a") and runs("out", i):
                    pe.wait_ge(s_side_read, nth(SIDES, i, ("back", 10)))
                    by_tokens(i, "out", mix_t, w_t[:, 3, :])
                if (t, where) == (11, "a") and runs("ffn", i):
                    pe.wait_ge(s_norm, nth(NORMS, i, "x2"))
                    transposes(i, "x2_t", normed_f)
                if (t, where) == (11, "b") and runs("ffn", i):
                    pe.wait_ge(s_act_job, nth(JOBS, i, "x2_t", "act"))
                    product(i, "q1", w_t[:, 0, :], normed_ft)

            def by_query(i, t):
                c, b, o = chunk(unit_stage(t), i), place(t), odd(unit_stage(t), i)
                if t in (5, 9):
                    k, q = ("k", "q") if t == 9 else ("k1", "q1")
                    pe.wait_ge(s_fill[k], 16 * (SP_FILLS + (t == 5)) * (c + 1))
                    pe.wait_ge(s_fill[q], 16 * SP_FILLS * (c + 1))
                    pe.wait_ge(s_pool_fill[k], 16 * POOL_FILLS * (c + 1))
                    pe.wait_ge(s_pool_fill[q], 16 * POOL_FILLS * (c + 1))
                for n in (0, 1):
                    n_before = 2 * (nth(UNITS, i, t) - 1) - 1 + n
                    if some(n_before):
                        pe.wait_ge(s_taken, n_before)
                    if layer(t) == 0:
                        nc.tensor.matmul(
                            query_bank[n][:].rearrange("p (a k) -> p a k", a=4)[:, :, 0:T], eye_query,
                            hide_key.unsqueeze(1).broadcast_to([P, 4, T]), start=True, stop=False,
                            skip_group_check=True)
                        for a in range(4):
                            g, half_of = 2 * n + a // 2, a % 2
                            ins = nc.tensor.matmul(
                                query_bank[n][:, a * P:(a + 1) * P],
                                q_stack[o][0:ROWS, g, b, P * half_of:P * half_of + P],
                                k_stack[o][0:ROWS, g, b, :], start=False, stop=(a == 3),
                                skip_group_check=True)
                    else:
                        s = 2 * b + n
                        for a in range(PAIRS):
                            ins = nc.tensor.matmul(
                                query_bank[n][:, a * T:(a + 1) * T],
                                q1_stack[:, a // 2, s, P * (a % 2):P * (a % 2) + P],
                                k1_stack[:, a // 2, s * T:(s + 1) * T], start=(a == 0), stop=(a == PAIRS - 1),
                                skip_group_check=True)
                    ins.then_inc(s_scores_q, 1)

            def by_key(i, t, n):
                b, o = place(t), odd(unit_stage(t), i)
                n_before = 2 * nth(UNITS, i, t) - 3 + n
                if some(n_before):
                    pe.wait_ge(s_probs, n_before)
                for m in (0, 1):
                    if layer(t) == 0:
                        nc.tensor.matmul(key_bank[n][:, 256 * m:256 * m + 256], k_stack[o][0:ROWS, 2 * n + m, b, :],
                                         q_stack[o][0:ROWS, 2 * n + m, b, :], start=(m == 0), stop=False,
                                         skip_group_check=True)
                    else:
                        for s in (0, 1):
                            at = 2 * b + s
                            nc.tensor.matmul(
                                key_bank[n][T * s:T * s + T, 256 * m:256 * m + 256],
                                k1_stack[:, 2 * n + m, at * T:(at + 1) * T], q1_stack[:, 2 * n + m, at, :],
                                start=(m == 0), stop=False, skip_group_check=True)
                pe.wait_ge(s_row, nth(UNITS, i, t))
                to_keys = C_S1 if layer(t) else C_S0
                for a in range(4 * n, 4 * n + 4):
                    ins = nc.tensor.matmul(key_bank[n][:, P * (a % 4):P * (a % 4) + P],
                                           spread[:, to_keys + P * a:to_keys + P * a + P], top_row[t % 2][:],
                                           start=False, stop=(a % 4 == 3), skip_group_check=True)
                ins.then_inc(s_scores_k, 1)

            def top_to_rows(i, t):
                pe.wait_ge(s_top, nth(UNITS, i, t))
                n_before = nth(UNITS, i, t) - 1
                if some(n_before):
                    pe.wait_ge(s_row, n_before)
                nc.tensor.transpose(turned, top_rep[t % 3][:], identity_b).then_inc(s_turned, 1)

            def to_tokens(i, t):
                pe.wait_ge(s_o_t, nth(UNITS, i, t) - 1 if runs(unit_stage(t), i) else nth(UNITS, i, t))
                n_before = nth(SIDES, i, ("nat", t)) - 1
                if some(n_before):
                    pe.wait_ge(s_side_read, n_before)
                for n in range(4):
                    ins = nc.tensor.transpose(side[:, n * P:(n + 1) * P], o_t[:, n].rearrange("p b q -> p (b q)"),
                                              identity)
                ins.then_inc(s_side, 1)

            def to_features(i, t):
                n_before = nth(SIDES, i, ("back", t)) - 1
                if some(n_before):
                    pe.wait_ge(s_side_read, n_before)
                for s in (0, 1):
                    ins = nc.tensor.transpose(side[:, s * P:(s + 1) * P], o_nat[:, s, :], identity)
                ins.then_inc(s_side, 1)

            def values(i, t, n):
                pe.wait_ge(s_probs, 2 * nth(UNITS, i, t) - 1 + n)
                if n == 0:
                    n_before = nth(UNITS, i, t) - 1
                    if some(n_before):
                        pe.wait_ge(s_o_t, n_before)
                    if ahead(i, t, 1):
                        pe.wait_ge(s_row, nth(UNITS, *ahead(i, t, 1)))
                pr, b = probs[t % 2], place(t)
                if layer(t) == 0:
                    for p in range(4 * n, 4 * n + 4):
                        j, a = p % 4, p // 4
                        ins = nc.tensor.matmul(
                            mixed[32 * j:32 * j + 32, P * a:P * a + P],
                            v0[odd(unit_stage(t), i)][:, b, 2 * p:2 * p + 2].rearrange("p s w -> p (s w)"),
                            pr[:, 2 * p:2 * p + 2].rearrange("p s q -> p (s q)"), start=True, stop=True)
                else:
                    for h in range(8 * n, 8 * n + 8):
                        j, g = h % 4, h // 4
                        ins = nc.tensor.matmul(
                            mixed[32 * j:32 * j + 32, T * g:T * g + T],
                            v1[:, b, h].rearrange("p s w -> p (s w)"), pr[:, h, :], start=True, stop=True)
                if n == 1:
                    ins.then_inc(s_mixed, 1)

            def body(i):
                for t in range(SLOTS):
                    unit = runs(unit_stage(t), i)
                    if (i.base, t) == (FIRST, 8):
                        pe.wait_ge(s_cast, 4)
                        pe.wait_ge(s_late, N_LATE)
                    start = (i.base, t) in STARTS
                    if start:
                        by_query(i, t + 1)
                        by_query(i, t + 2)
                        top_to_rows(i, t + 1)
                    if t in NAT and runs(NAT[t], i):
                        to_tokens(i, t)
                    if t in BACK and runs("out", i):
                        to_features(i, t)
                    dense(i, t, "a")
                    if (unit or start) and ahead(i, t, 3):
                        by_query(*ahead(i, t, 3))
                    for n in (0, 1):
                        if (unit or start) and ahead(i, t, 1):
                            by_key(*ahead(i, t, 1), n)
                        if unit:
                            values(i, t, n)
                    if (unit or start) and ahead(i, t, 2):
                        top_to_rows(*ahead(i, t, 2))
                    dense(i, t, "b")
                    if (i.base, t) == (FIRST, 11):
                        for n in range(4):
                            ins = nc.tensor.transpose(dense_bank[1][:, n * D:(n + 1) * D], w_nat[:, n * D:(n + 1) * D],
                                                      identity)
                        ins.then_inc(s_wt, 1)
                        pe.wait_ge(s_wt_read, 1)

            pipeline(pe, body)

        @block.vector
        def _(dve):
            steps = [0]

            def step(ins):
                steps[0] += 1
                ins.then_inc(s_step, 1)
                dve.wait_ge(s_step, steps[0])

            def set_up():
                dve.wait_ge(s_const, N_CONST)
                dve.wait_ge(s_late, N_LATE)
                nc.vector.tensor_copy(cstb[:], cst[:, CW:CW + CWB]).then_inc(s_cast, 1)
                nc.vector.tensor_copy(spread[:], spread_in[:].rearrange("p a b -> p (a b)")).then_inc(s_cast, 1)
                for n in (0, 1):
                    nc.vector.tensor_copy(top_row[n][T:P], cst[T:P, CW + C_HQ:CW + C_HQ + 2 * T]).then_inc(s_cast, 1)

            for n, (dst, value) in enumerate(memsets):
                nc.vector.memset(dst, value).then_inc(s_setup, 1)
                dve.wait_ge(s_setup, n + 1)

            def job(i, name):
                dve.wait_ge(s_job, nth(JOBS, i, name))
                return dense_bank[BANK[name]]

            def flat(a):
                return a[:].rearrange("p t d -> p (t d)")

            def norm_stats(i, name, src):
                for t in range(TILES):
                    ins = nc.vector.bn_stats(stat6[:, t, :], src[:, t, :])
                step(ins)
                for t in range(TILES):
                    ins = nc.vector.bn_aggr(mean_var[name][:, t, :], stat6[:, t, :])
                step(ins)
                nc.vector.tensor_scalar(var_eps[name][:], mean_var[name][:, :, 1], EPS, None,
                                        ALU.add).then_inc(s_var, 1)

            def norm_rows(i, name, src, dst):
                dve.wait_ge(s_rstd, nth(NORMS, i, name))
                for t in range(TILES):
                    ins = nc.vector.tensor_scalar(dst[:, t, :], src[:, t, :], mean_var[name][:, t, 0:1],
                                                  rstd[name][:, t:t + 1], ALU.subtract, ALU.mult)
                ins.then_inc(s_norm, 1)

            def low(i, name, src, bias, hi, lo):
                dve.wait_ge(s_hi, nth(HIGHS, i, name))
                nc.vector.scalar_tensor_tensor(out=lo, in0=src, scalar=cols[:, bias:bias + 1], in1=hi, op0=ALU.add,
                                               op1=ALU.subtract).then_inc(s_dve_job, 1)

            def diagonal(a):
                for s in range(HG):
                    ins = nc.vector.tensor_scalar(
                        q_diag[:, a, :, s, :], q_part[:, a, :].rearrange("p (b q) -> p b q", q=T),
                        hh_mask[:, s:s + 1], None, ALU.mult)
                ins.then_inc(s_diag if a else s_diag_hi, 1)

            def take_top(i, t):
                dve.wait_ge(s_scores_q, 2 * nth(UNITS, i, t) - 1)
                w = 4 if layer(t) == 0 else 8
                maxima = top[t % 2][:].rearrange("p n a -> p (n a)")
                for n in (0, 1):
                    if n == 1:
                        dve.wait_ge(s_scores_q, 2 * nth(UNITS, i, t))
                    nc.vector.tensor_reduce(maxima[:, w * n:w * n + w],
                                            query_bank[n][:].rearrange("p (a k) -> p a k", a=w), AX_X, ALU.max,
                                            negate=True).then_inc(s_taken, 1)
                dve.wait_ge(s_taken, 2 * nth(UNITS, i, t))
                step(nc.vector.tensor_copy(top_rep[t % 3][:, 0:2 * w], maxima[:, 0:2 * w]))
                nc.vector.tensor_tensor(top_rep[t % 3][:, 2 * w:4 * w], maxima[:, 0:2 * w],
                                        top_rep[t % 3][:, 0:2 * w], ALU.subtract).then_inc(s_top, 1)

            def normalize(i, t):
                dve.wait_ge(s_side, nth(SIDES, i, ("nat", t)))
                if layer(t - 1) == 0:
                    o, tile = odd(NAT[t], i), place(t - 1) // 2
                    nat = side[:].rearrange("p (s e) -> p s e", s=2)
                    for s in (0, 1):
                        ins = nc.vector.reciprocal(rden[:, 8 * s:8 * s + 8], nat[:, s, VW * s + DH:256:32])
                    step(ins)
                    for s in (0, 1):
                        num = nat[:, s].rearrange("p (a w) -> p a w", w=32)[:, :, VW * s:VW * s + DH]
                        ins = nc.vector.tensor_tensor(
                            o_nat[:, 0, :].rearrange("p (a s d) -> p a s d", s=2, d=DH)[:, :, s, :], num,
                            rden[:, 8 * s:8 * s + 8].unsqueeze(2).broadcast_to([P, PAIRS, DH]), ALU.mult)
                    ins.then_inc(s_side_read, 1)
                    dve.wait_ge(s_side_read, nth(SIDES, i, ("nat", t)))
                    nc.vector.tensor_tensor(x1[o][:, tile, :], x_in[o][:, tile, :], o_nat[:, 0, :],
                                            ALU.add).then_inc(s_x1, 1)
                else:
                    nat = side[:].rearrange("p (h s w) -> p h s w", h=H, s=2)
                    both = rden[:].rearrange("p (h s) -> p h s", s=2)
                    step(nc.vector.reciprocal(both, nat[:, :, :, DH]))
                    for s in (0, 1):
                        ins = nc.vector.tensor_tensor(
                            o_nat[:, s, :].rearrange("p (h d) -> p h d", d=DH), nat[:, :, s, 0:DH],
                            both[:, :, s].unsqueeze(2).broadcast_to([P, H, DH]), ALU.mult)
                    ins.then_inc(s_side_read, 1)

            def transferred(stack, chunks):
                dve.wait_ge(s_fill[stack], 16 * SP_FILLS * chunks)
                dve.wait_ge(s_pool_fill[stack], 16 * POOL_FILLS * chunks)

            def by_key_rows(a):
                return a.rearrange("p (b k) -> p b k", k=T)

            def dense(i, t, where):
                o, f = odd("in", i), odd("ffn", i)
                if (t, where) == (0, "b") and runs("in", i):
                    dve.wait_ge(s_x, 16 * (chunk("in", i) + 1))
                    norm_stats(i, "x", x_in[o])
                if (t, where) == (1, "a") and runs("in", i):
                    if i.base > FIRST:
                        dve.wait_ge(s_job, nth(JOBS, after(i, -1), "q1"))
                    norm_rows(i, "x", x_in[o], normed)
                if (t, where) == (2, "a") and runs("in", i):
                    low(i, "k_ctx", by_key_rows(job(i, "k_ctx")[:]), BKC, k_part[:, 0, :, 1, :], k_part[:, 1, :, 1, :])
                if (t, where) == (3, "a") and runs("in", i):
                    low(i, "k0", by_key_rows(job(i, "k0")[:]), BK0, k_part[:, 0, :, 0, :], k_part[:, 1, :, 0, :])
                if (t, where) == (3, "b") and runs("in", i):
                    if i.base > 0:
                        transferred("q1", chunk("out", i) + 1)
                    elif i.base > FIRST:
                        transferred("q", chunk("in", i))
                    dve.wait_ge(s_hi, nth(HIGHS, i, "q0"))
                    diagonal(0)
                    low(i, "q0", job(i, "q0")[:], BQ0, q_part[:, 0], q_part[:, 1])
                    dve.wait_ge(s_dve_job, nth(JOBS, i, "q0", "dve"))
                    diagonal(1)
                if t == 4 and runs("in", i):
                    name, b = ("v0a", 0) if where == "a" else ("v0b", 4)
                    nc.vector.tensor_tensor(
                        v0[o][:, b:b + 4, :, 0:DH], job(i, name)[:].rearrange("p (b h d) -> p b h d", b=4, d=DH),
                        row_bv0[:].rearrange("p (h d) -> p h d", d=DH).unsqueeze(1).broadcast_to([P, 4, H, DH]),
                        ALU.add).then_inc(s_dve_job, 1)
                if (t, where) == (5, "a") and runs("ffn", i):
                    dve.wait_ge(s_x1, nth(RESIDUALS, i, 5))
                    norm_stats(i, "x1", x1[f])
                if (t, where) == (5, "b") and runs("ffn", i):
                    if i.base > 0:
                        dve.wait_ge(s_job, nth(JOBS, after(i, -1), "q1"))
                    norm_rows(i, "x1", x1[f], normed_f)
                if (t, where) == (6, "a") and runs("ffn", i):
                    if i.base > 0:
                        dve.wait_ge(s_hi, nth(HIGHS, after(i, -1), "k1"))
                    dve.wait_ge(s_pool, nth(POOLED, i, "keep"))
                    nc.vector.scalar_tensor_tensor(
                        out=k1_full[:], in0=job(i, "k1")[:], scalar=cols[:, BK1:BK1 + 1], in1=keep[:], op0=ALU.add,
                        op1=ALU.mult).then_inc(s_dve_job, 1)
                if (t, where) == (6, "b") and runs("ffn", i):
                    dve.wait_ge(s_pool, nth(POOLED, i, "offset"))
                    norm_stats(i, "x1_again", normed_f)
                if (t, where) == (7, "a") and runs("ffn", i):
                    norm_rows(i, "x1_again", normed_f, normed_f)
                if (t, where) == (8, "b") and runs("ffn", i):
                    dve.wait_ge(s_scores_k, 2 * nth(UNITS, i, 8))
                    dve.wait_ge(s_hi, nth(HIGHS, i, "k1"))
                    nc.vector.tensor_tensor(k1_part[:, 1], k1_full[:], k1_part[:, 0], ALU.subtract).then_inc(s_k1_lo, 1)
                if (t, where) == (9, "b") and runs("ffn", i):
                    dve.wait_ge(s_pool, nth(POOLED, i, "x1_b2"))
                    nc.vector.tensor_tensor(flat(x2[f]), job(i, "w2")[:], flat(x1[f]), ALU.add).then_inc(s_dve_job, 1)
                    dve.wait_ge(s_dve_job, nth(JOBS, i, "w2", "dve"))
                    norm_stats(i, "x2", x2[f])
                if (t, where) == (10, "a") and runs("ffn", i):
                    norm_rows(i, "x2", x2[f], normed_f)
                if (t, where) == (11, "a") and runs("out", i):
                    dve.wait_ge(s_pool, nth(POOLED, after(i, -1), "x2_bo"))
                    if i.base > 1 or i.reg is not None:
                        dve.wait_ge(s_stored, 16 * (chunk("out", i) + 1))
                    nc.vector.tensor_tensor(flat(result), job(i, "out")[:], flat(x2[odd("out", i)]),
                                            ALU.add).then_inc(s_dve_job, 1)
                if (t, where) == (11, "b") and runs("ffn", i):
                    transferred("q", chunk("in", i) + 1 if runs("in", i) else CHUNKS)
                    dve.wait_ge(s_hi, nth(HIGHS, i, "q1"))
                    diagonal(0)
                    low(i, "q1", job(i, "q1")[:], BQ1, q_part[:, 0], q_part[:, 1])
                    dve.wait_ge(s_dve_job, nth(JOBS, i, "q1", "dve"))
                    diagonal(1)

            def body(i):
                steps[0] = 0
                for t in range(SLOTS):
                    unit = runs(unit_stage(t), i) or (i.base, t) in STARTS
                    if (i.base, t) == (FIRST, 8):
                        set_up()
                    if (i.base, t) in STARTS:
                        take_top(i, t + 1)
                        take_top(i, t + 2)
                    if t in NAT and runs(NAT[t], i):
                        normalize(i, t)
                    dense(i, t, "a")
                    if unit and ahead(i, t, 3):
                        take_top(*ahead(i, t, 3))
                    dense(i, t, "b")
                dve.sem_clear(s_step)

            pipeline(dve, body)


_INS = ["x", "ctx_1024", "mask_BxS2_ik0", "L0_xattn_w_qkv", "L0_xattn_b_qkv", "L0_xattn_w_ckv", "L0_xattn_b_ckv",
        "L0_xattn_g1", "L0_xattn_be1", "L0_xattn_g2", "L0_xattn_be2", "L0_xattn_gf", "L0_xattn_bf", "L0_xattn_w1",
        "L0_xattn_b1", "L0_xattn_w2", "L0_xattn_b2", "L1_xattn_ln_w", "L1_xattn_ln_b", "L1_xattn_wq", "L1_xattn_bq",
        "L1_xattn_wk", "L1_xattn_bk", "L1_xattn_wv", "L1_xattn_bv", "L1_xattn_wo", "L1_xattn_bo"]


def kernel(**inputs):
    import numpy as _np
    import concourse.bacc as _bacc
    from concourse import mybir as _mybir
    from concourse.bass_utils import run_bass_kernel_spmd as _run

    nc = _bacc.Bacc("TRN2", target_bir_lowering=False, num_devices=1)
    arrays, io = {}, {}
    for name in _INS + ["constants"]:
        a = _np.ascontiguousarray(constants() if name == "constants" else inputs[name])
        arrays[f"in_{name}"] = a
        io[name] = nc.dram_tensor(f"in_{name}", a.shape, _mybir.dt.from_np(a.dtype), kind="ExternalInput").ap()
    out = nc.dram_tensor("out_0", (B, T, D), F32, kind="ExternalOutput").ap()
    xattn_program(nc, io, io.pop("constants"), out)
    r = _run(nc, [arrays], core_ids=[0])
    return r.results[0]["out_0"]
```
